# Optimizing a Trainium2 kernel written in Bass

```python
import numpy as np
import jax
import jax.numpy as jnp

def _softmax(x, axis=-1):
    return jax.nn.softmax(x, axis=axis)

def _gelu(x):
    return jax.nn.gelu(x, approximate=True)

def _silu(x):
    return jax.nn.silu(x)

def _sigmoid(x):
    return jax.nn.sigmoid(x)

def _layernorm(x, axis=-1, eps=1e-05):
    m = jnp.mean(x, axis=axis, keepdims=True)
    v = jnp.var(x, axis=axis, keepdims=True)
    return (x - m) / jnp.sqrt(v + eps)

def _scatter_add(tgt, idx, src, axis=0):
    return tgt.at[idx].add(src)

def _segment_sum(src, seg, n):
    return jax.ops.segment_sum(src, seg, n)
kernel_name = 'mk_decoder_postln_d1_seqx_r8_7327cc'

def setup_inputs(seed: int=0):
    np.random.seed(seed)
    _w = jnp.asarray

    def _rec_inputs():
        import jax
        import jax.numpy as jnp
        _rk = jax.random.key(seed)
        x = -0.000929 + 1 * jax.random.normal(jax.random.fold_in(_rk, 1), (4, 256, 128), jnp.float32)
        _lenS = 256 - jax.random.randint(jax.random.fold_in(_rk, 7), (4,), 0, max(1, 256 // 4) + 1, jnp.int32)
        _lenS2 = 1601 - jax.random.randint(jax.random.fold_in(_rk, 8), (4,), 0, max(1, 1601 // 4) + 1, jnp.int32)
        _ctx_1024P = jax.random.normal(jax.random.fold_in(_rk, 11), (4, 16, 128), jnp.float32)
        _ctx_1024c = jax.random.dirichlet(jax.random.fold_in(_rk, 511), 0.3 * jnp.ones((16,), jnp.float32), (4, 1601))
        _ctx_1024t = jnp.einsum('bsk,bkd->bsd', _ctx_1024c, _ctx_1024P)
        _ctx_1024t = _ctx_1024t * jax.lax.rsqrt(jnp.mean(jnp.square(_ctx_1024t)) + 1e-12) * 0.953939
        ctx_1024 = 0.000227908 + 0.99994 * (_ctx_1024t + 0.3 * jax.random.normal(jax.random.fold_in(_rk, 611), (4, 1601, 128), jnp.float32))
        fside_BxSxS2_0 = jax.random.uniform(jax.random.fold_in(_rk, 12), (4, 256, 1601), jnp.float32, 0.0, 0.999998)
        _validS = jnp.arange(256)[None, :] < _lenS[:, None]
        _validS2 = jnp.arange(1601)[None, :] < _lenS2[:, None]
        _causal = jnp.tril(jnp.ones((256, 256), dtype=bool))
        mask_Bx1x1xS2_ff0 = jnp.where(jnp.ones((4, 1, 1, 1601), dtype=bool), 0.0, -1000000000.0).astype(jnp.float32)
        return (x, ctx_1024, fside_BxSxS2_0, mask_Bx1x1xS2_ff0)
    x, ctx_1024, fside_BxSxS2_0, mask_Bx1x1xS2_ff0 = _rec_inputs()

    def _L0_attn_setup():
        import jax, jax.numpy as jnp
        import numpy as np
        import math
        B, T, D, H = (2, 256, 128, 16)
        DH = D // H

        def rotate_half(x):
            x1 = x[..., ::2]
            x2 = x[..., 1::2]
            return jnp.stack((-x2, x1), axis=-1).reshape(x.shape)
        key = jax.random.key(seed)
        k1, k2, k3 = jax.random.split(key, 3)
        x = jax.random.normal(k1, (B, T, D), dtype=jnp.float32)
        Wqkv = jax.random.normal(k2, (3 * D, D), dtype=jnp.float32) * (1.0 / math.sqrt(D))
        Wo = jax.random.normal(k3, (D, D), dtype=jnp.float32) * (1.0 / math.sqrt(D))
        return {'x': x, 'Wqkv': Wqkv, 'Wo': Wo}
    _L0_attn_all = _L0_attn_setup()
    _L0_attn_in = {k: v for k, v in _L0_attn_all.items() if k in ('Wqkv', 'Wo')}
    del _L0_attn_all

    def _L0_xattn_setup():
        import jax, jax.numpy as jnp
        import numpy as np
        B, F, T = (2, 64, 64)
        D, N, H = (128, 16, 64)
        K = 32
        FILT = 512
        L = 4
        EPS = 1e-06

        def _glorot(key, shape, fan_in, fan_out):
            lim = np.sqrt(6.0 / (fan_in + fan_out)).astype(np.float32)
            return jax.random.uniform(key, shape, jnp.float32, -lim, lim)

        def _norm(x):
            m = jnp.mean(x, axis=-1, keepdims=True)
            s = jnp.sqrt(jnp.mean((x - m) ** 2, axis=-1, keepdims=True))
            return (x - m) / (s + EPS)

        def _attention(x, src, dist, bias, Wq, Wk, Wv, Wo, Wth, bth, Wto, bto):
            q = jnp.einsum('bfd,dnh->bfnh', x, Wq) * H ** (-0.5)
            k = jnp.einsum('btd,dnh->btnh', src, Wk)
            v = jnp.einsum('btd,dnh->btnh', src, Wv)
            hbias = jax.nn.relu(dist[..., None] @ Wth + bth)
            qs_bias = (hbias @ Wto + bto)[..., 0]
            logits = jnp.einsum('btnh,bfnh->bnft', k, q)
            logits = logits + bias + qs_bias[:, None]
            w = jax.nn.softmax(logits, axis=-1)
            out = jnp.einsum('bnft,btnh->bfnh', w, v)
            return jnp.einsum('bfnh,nhd->bfd', out, Wo)
        key = jax.random.key(seed)
        ks = jax.random.split(key, 18)
        inp = {'decoder_inputs': jax.random.normal(ks[0], (B, F, D), jnp.float32), 'encoder_outputs': jax.random.normal(ks[1], (B, T, D), jnp.float32), 'decoder_times_dist': jax.random.uniform(ks[2], (B, F, F), jnp.float32), 'decoder_encoder_times_dist': jax.random.uniform(ks[3], (B, F, T), jnp.float32), 'dec_self_attn_bias': jnp.zeros((B, 1, 1, F), jnp.float32), 'enc_dec_attn_bias': jnp.zeros((B, 1, 1, T), jnp.float32), 'Wq': _glorot(ks[4], (L, D, N, H), D, D), 'Wk': _glorot(ks[5], (L, D, N, H), D, D), 'Wv': _glorot(ks[6], (L, D, N, H), D, D), 'Wo': _glorot(ks[7], (L, N, H, D), D, D), 'Wth': _glorot(ks[8], (L, 1, K), 1, K), 'bth': jnp.zeros((L, K), jnp.float32), 'Wto': _glorot(ks[9], (L, K, 1), K, 1), 'bto': jnp.zeros((L, 1), jnp.float32), 'Wf1': _glorot(ks[10], (L, D, FILT), D, FILT), 'bf1': jnp.zeros((L, FILT), jnp.float32), 'Wf2': _glorot(ks[11], (L, FILT, D), FILT, D), 'bf2': jnp.zeros((L, D), jnp.float32)}
        return inp
    _L0_xattn_all = _L0_xattn_setup()
    _L0_xattn_in = {k: v for k, v in _L0_xattn_all.items() if k in ('Wq', 'Wk', 'Wv', 'Wo', 'Wth', 'bth', 'Wto', 'bto', 'Wf1', 'bf1', 'Wf2', 'bf2')}
    del _L0_xattn_all

    def _L0_ffn_setup():
        import jax, jax.numpy as jnp
        import numpy as np
        B, T, C, H, E = (4, 256, 128, 256, 8)
        CAPACITY_FACTOR = 1.0
        key = jax.random.key(seed)
        ks = jax.random.split(key, 5)
        scale = 0.02
        return {'x': jax.random.normal(ks[0], (B, T, C), dtype=jnp.float32), 'Wg': jax.random.normal(ks[1], (E, C), dtype=jnp.float32) * scale, 'W1': jax.random.normal(ks[2], (E, H, C), dtype=jnp.float32) * scale, 'W2': jax.random.normal(ks[3], (E, C, H), dtype=jnp.float32) * scale, 'W3': jax.random.normal(ks[4], (E, H, C), dtype=jnp.float32) * scale}
    _L0_ffn_all = _L0_ffn_setup()
    _L0_ffn_in = {k: v for k, v in _L0_ffn_all.items() if k in ('Wg', 'W1', 'W2', 'W3')}
    del _L0_ffn_all
    return {'x': x, 'ctx_1024': ctx_1024, 'fside_BxSxS2_0': fside_BxSxS2_0, 'mask_Bx1x1xS2_ff0': mask_Bx1x1xS2_ff0, 'L0_attn_Wqkv': _L0_attn_in['Wqkv'], 'L0_attn_Wo': _L0_attn_in['Wo'], 'L0_xattn_Wq': _L0_xattn_in['Wq'], 'L0_xattn_Wk': _L0_xattn_in['Wk'], 'L0_xattn_Wv': _L0_xattn_in['Wv'], 'L0_xattn_Wo': _L0_xattn_in['Wo'], 'L0_xattn_Wth': _L0_xattn_in['Wth'], 'L0_xattn_bth': _L0_xattn_in['bth'], 'L0_xattn_Wto': _L0_xattn_in['Wto'], 'L0_xattn_bto': _L0_xattn_in['bto'], 'L0_xattn_Wf1': _L0_xattn_in['Wf1'], 'L0_xattn_bf1': _L0_xattn_in['bf1'], 'L0_xattn_Wf2': _L0_xattn_in['Wf2'], 'L0_xattn_bf2': _L0_xattn_in['bf2'], 'L0_ffn_Wg': _L0_ffn_in['Wg'], 'L0_ffn_W1': _L0_ffn_in['W1'], 'L0_ffn_W2': _L0_ffn_in['W2'], 'L0_ffn_W3': _L0_ffn_in['W3']}

def reference(x, ctx_1024, fside_BxSxS2_0, mask_Bx1x1xS2_ff0, L0_attn_Wqkv, L0_attn_Wo, L0_xattn_Wq, L0_xattn_Wk, L0_xattn_Wv, L0_xattn_Wo, L0_xattn_Wth, L0_xattn_bth, L0_xattn_Wto, L0_xattn_bto, L0_xattn_Wf1, L0_xattn_bf1, L0_xattn_Wf2, L0_xattn_bf2, L0_ffn_Wg, L0_ffn_W1, L0_ffn_W2, L0_ffn_W3):
    import jax
    import jax.numpy as jnp

    def _L0_attn_ref(x, Wqkv, Wo):
        import jax, jax.numpy as jnp
        import numpy as np
        import math
        B, T, D, H = (2, 256, 128, 16)
        DH = D // H

        def rotate_half(x):
            x1 = x[..., ::2]
            x2 = x[..., 1::2]
            return jnp.stack((-x2, x1), axis=-1).reshape(x.shape)
        b, t, d = x.shape
        pos = jnp.arange(t, dtype=jnp.float32)
        freqs = jnp.exp(-math.log(10000.0) * jnp.arange(0, DH, 2, dtype=jnp.float32) / DH)
        angles = pos[:, None] * freqs[None, :]
        angles = jnp.repeat(angles, 2, axis=-1)
        sin = jnp.sin(angles)[None, None, :, :]
        cos = jnp.cos(angles)[None, None, :, :]
        qkv = x @ Wqkv.T
        q, k, v = jnp.split(qkv, 3, axis=-1)
        q = q.reshape(b, t, H, DH).transpose(0, 2, 1, 3)
        k = k.reshape(b, t, H, DH).transpose(0, 2, 1, 3)
        v = v.reshape(b, t, H, DH).transpose(0, 2, 1, 3)
        q = cos * q + rotate_half(q) * sin
        k = cos * k + rotate_half(k) * sin
        scores = jnp.einsum('bhqd,bhkd->bhqk', q, k) / math.sqrt(DH)
        causal = jnp.tril(jnp.ones((t, t), dtype=bool))
        scores = jnp.where(causal, scores, -jnp.inf)
        attn = jax.nn.softmax(scores, axis=-1)
        out = jnp.einsum('bhqk,bhkd->bhqd', attn, v)
        out = out.transpose(0, 2, 1, 3).reshape(b, t, d)
        return out @ Wo.T

    def _L0_xattn_ref(decoder_inputs, encoder_outputs, decoder_times_dist, decoder_encoder_times_dist, dec_self_attn_bias, enc_dec_attn_bias, Wq, Wk, Wv, Wo, Wth, bth, Wto, bto, Wf1, bf1, Wf2, bf2):
        import jax, jax.numpy as jnp
        import numpy as np
        B, F, T = (2, 64, 64)
        D, N, H = (128, 16, 64)
        K = 32
        FILT = 512
        L = 4
        EPS = 1e-06

        def _glorot(key, shape, fan_in, fan_out):
            lim = np.sqrt(6.0 / (fan_in + fan_out)).astype(np.float32)
            return jax.random.uniform(key, shape, jnp.float32, -lim, lim)

        def _norm(x):
            m = jnp.mean(x, axis=-1, keepdims=True)
            s = jnp.sqrt(jnp.mean((x - m) ** 2, axis=-1, keepdims=True))
            return (x - m) / (s + EPS)

        def _attention(x, src, dist, bias, Wq, Wk, Wv, Wo, Wth, bth, Wto, bto):
            q = jnp.einsum('bfd,dnh->bfnh', x, Wq) * H ** (-0.5)
            k = jnp.einsum('btd,dnh->btnh', src, Wk)
            v = jnp.einsum('btd,dnh->btnh', src, Wv)
            hbias = jax.nn.relu(dist[..., None] @ Wth + bth)
            qs_bias = (hbias @ Wto + bto)[..., 0]
            logits = jnp.einsum('btnh,bfnh->bnft', k, q)
            logits = logits + bias + qs_bias[:, None]
            w = jax.nn.softmax(logits, axis=-1)
            out = jnp.einsum('bnft,btnh->bfnh', w, v)
            return jnp.einsum('bfnh,nhd->bfd', out, Wo)
        x = decoder_inputs
        for i in range(L):
            y = _attention(_norm(x), encoder_outputs, decoder_encoder_times_dist, enc_dec_attn_bias, Wq[i], Wk[i], Wv[i], Wo[i], Wth[i], bth[i], Wto[i], bto[i])
            x = x + y
            y = jax.nn.relu(_norm(x) @ Wf1[i] + bf1[i]) @ Wf2[i] + bf2[i]
            x = x + y
        return _norm(x)

    def _L0_ffn_ref(x, Wg, W1, W2, W3):
        import jax, jax.numpy as jnp
        import numpy as np
        B, T, C, H, E = (4, 256, 128, 256, 8)
        CAPACITY_FACTOR = 1.0
        b, t, c = x.shape
        e = Wg.shape[0]
        n = b * t
        capacity = max(1, int(CAPACITY_FACTOR * n / e))
        x_flat = x.reshape(n, c)
        scores = (x_flat @ Wg.T).T
        top_vals, token_idx = jax.lax.top_k(scores, capacity)
        token_w = jax.nn.softmax(top_vals, axis=-1)
        xg = x_flat[token_idx]
        h = jax.nn.silu(jnp.einsum('eic,ehc->eih', xg, W1)) * jnp.einsum('eic,ehc->eih', xg, W3)
        y = jnp.einsum('eih,ech->eic', h, W2) * token_w[..., None]
        out = jnp.zeros_like(x_flat).at[token_idx.reshape(-1)].add(y.reshape(-1, c))
        return out.reshape(b, t, c)
    x = _layernorm(x + _L0_attn_ref(x, L0_attn_Wqkv, L0_attn_Wo), axis=-1)
    x = _layernorm(x + _L0_xattn_ref(x, ctx_1024, fside_BxSxS2_0, fside_BxSxS2_0, mask_Bx1x1xS2_ff0, mask_Bx1x1xS2_ff0, L0_xattn_Wq, L0_xattn_Wk, L0_xattn_Wv, L0_xattn_Wo, L0_xattn_Wth, L0_xattn_bth, L0_xattn_Wto, L0_xattn_bto, L0_xattn_Wf1, L0_xattn_bf1, L0_xattn_Wf2, L0_xattn_bf2), axis=-1)
    x = _layernorm(x + _L0_ffn_ref(x, L0_ffn_Wg, L0_ffn_W1, L0_ffn_W2, L0_ffn_W3), axis=-1)
    return x

_drawn_inputs = setup_inputs


def setup_inputs(seed=0):
    import zlib

    import numpy as np

    out = dict(_drawn_inputs(seed))
    spreads = {'L0_xattn_bth': (0.0, 0.8),
     'L0_xattn_bto': (0.0, 0.8),
     'L0_xattn_bf1': (0.0, 0.1),
     'L0_xattn_bf2': (0.0, 0.1)}
    factors = {'fside_BxSxS2_0': 8.0,
     'L0_xattn_Wth': 8.0,
     'L0_xattn_Wto': 8.0,
     'L0_ffn_Wg': 8.0,
     'L0_ffn_W1': 8.0,
     'L0_ffn_W2': 8.0,
     'L0_ffn_W3': 8.0}
    for name, (base, spread) in spreads.items():
        noise = np.random.default_rng([zlib.crc32(name.encode()), seed]).standard_normal(out[name].shape)
        drawn = base * np.exp(spread * noise) if base else spread * noise
        out[name] = jnp.asarray(drawn.astype(out[name].dtype))
    for name, factor in factors.items():
        out[name] = (out[name] * factor).astype(out[name].dtype)
    return out
```

```python
from contextlib import ExitStack

import concourse.bass as bass
from concourse import mybir

F32 = mybir.dt.float32
ALU = mybir.AluOpType
ACT = mybir.ActivationFunctionType

P = 128
B, S, D, T = 4, 256, 128, 1601
FT = S // P
L, HEADS, HD, HID = 4, 16, 64, 32
STEPS = L * B
PAIRS = HEADS // 2
UNITS = HEADS * FT
TT = -(-T // P)
LAST = T - (TT - 1) * P
TG = 4
CUT = 1024
FILT, FB = 512, 4
SH, SHD, GH = 16, 8, 4
SG = SH // GH
E, EH, CAP = 8, 256, 128
TOK = B * S
TILES = TOK // P
BIG = 3.0e38

START = ["XN1", "Q0", "QK", "V0", "V1", "V2"]
FIRST = [("V3", None, "Q"), ("QK", None, "V0"), ("V1", "PV", None), ("V2", "PV", None)]
MIDDLE = [("V3", "PV", "Q"), ("QK", "PV", "V0"), ("OT", "PV", "V1"), ("Y", "PV", "V2")]
FINAL = [("V3", "PV", None), (None, "PV", None), ("OT", "PV", None), ("Y", "PV", None)]
TAIL = ["PV", "PV", "OT", "Y0", "XN2", "H0", "H1", "Y2"]


def flat(kind):
    return [name for slot in kind for name in slot if name]


BASE_FIRST = len(START)
PER_PAIR = len(flat(MIDDLE))
BASE_MIDDLE = BASE_FIRST + len(flat(FIRST)) - PER_PAIR
BASE_TAIL = BASE_MIDDLE + PER_PAIR * (PAIRS - 1) + len(flat(FINAL))
TASKS = BASE_TAIL + len(TAIL)
assert BASE_FIRST % 2 == BASE_MIDDLE % 2 == PER_PAIR % 2 == 0
NORMS = 2
CHAIN_SA = 3 + 4
CHAIN_STEP = 2 * 4 + 1


QK_AT = flat(MIDDLE).index("QK")


def pairs_of(s, emit, each_j):
    emit(s, 0, 0, FIRST, BASE_FIRST, 2)
    emit(s, 1, 1, MIDDLE, BASE_MIDDLE + PER_PAIR, BASE_FIRST + flat(FIRST).index("QK"))
    with each_j(1, PAIRS // 2 - 1) as j:
        for half in range(2):
            p = 2 * j + half
            emit(s, p, half, MIDDLE, BASE_MIDDLE + PER_PAIR * p, BASE_MIDDLE + PER_PAIR * (p - 1) + QK_AT)
    for p, kind in ((PAIRS - 2, MIDDLE), (PAIRS - 1, FINAL)):
        emit(s, p, p % 2, kind, BASE_MIDDLE + PER_PAIR * p, BASE_MIDDLE + PER_PAIR * (p - 1) + QK_AT)


def pair_of(name, p, parity):
    if name in ("Q", "QK", "V0", "V1", "V2"):
        return p + 1, 1 - parity
    if name in ("OT", "Y"):
        return p - 1, 1 - parity
    return p, parity


def weights_row(s, p):
    step, pair = (s, p) if p < PAIRS else (s + 1, p - PAIRS)
    return (step // B * PAIRS + pair) % (L * PAIRS)


def build(nc, d):
    with ExitStack() as ctx:
        def sb(name, shape):
            return ctx.enter_context(nc.sbuf_tensor(name, shape, F32))

        def sem(name):
            return ctx.enter_context(nc.semaphore(name))

        psum = ctx.enter_context(nc.psum_tensor("banks", [P, 8, 512], F32))

        ident = sb("ident", [P, P])
        half = sb("half", [P, 8])
        coef = sb("coef", [P, 2, (STEPS + 1) * HID])
        negc = sb("negc", [P, (STEPS + 1) * HID])
        nbto = sb("nbto", [P, STEPS + 1])
        xs = sb("xs", [P, STEPS + B, FT, D])
        dist = sb("dist", [P, 2, FT, T])
        maskb = sb("maskb", [P, T])
        nmask = sb("nmask", [P, T])
        relu = sb("relu", [P, 2, FT, T])
        nb_next = sb("nb_next", [P, FT, T])
        nb_cur = sb("nb_cur", [P, FT, T])
        ctxT = sb("ctxT", [P, T])
        prob = sb("prob", [P, 2, T])
        probT = sb("probT", [P, 2, TT, P])
        val = sb("val", [P, 2, TT, P])
        wqkv = sb("wqkv", [P, 2, 3, P])
        wo = sb("wo", [P, 2, P])
        wf1 = sb("wf1", [P, FILT])
        wf2 = sb("wf2", [P, FB, D])
        bf1 = sb("bf1", [P, FB])
        bf2 = sb("bf2", [P, D])
        xcur = sb("xcur", [P, FT, D])
        xn = sb("xn", [P, FT, D])
        xnT = sb("xnT", [P, S])
        q_sb = sb("q_sb", [P, 2, S])
        qk_sb = sb("qk_sb", [P, 2, 2, S])
        nmA = sb("nmA", [P, 4])
        nm = sb("nm", [P, 4])
        rsum = sb("rsum", [P, 4])
        rinv = sb("rinv", [P, 4])
        On = sb("On", [P, 2, FT, P])
        OT = sb("OT", [P, S])
        hT = sb("hT", [P, FB, S])
        bn = sb("bn", [P, TILES, 6])
        mv = sb("mv", [P, TILES, 2])
        vv = sb("vv", [P, TILES])
        sd = sb("sd", [P, TILES])
        rs = sb("rs", [P, TILES])

        def sems(*names):
            return [sem(n) for n in names]

        (const_ld, coef_ld, x_ld, xT_ld, out_st) = sems("const_ld", "coef_ld", "x_ld", "xT_ld", "out_st")
        (dist_ld, gate_ld, sa_ri, mo_n, carried) = sems("dist_ld", "gate_ld", "sa_ri", "mo_n", "carried")
        w_ld = sems("w_ld0", "w_ld1")
        wo_ld = sems("wo_ld0", "wo_ld1")
        (mask_ld, ctx_ld, ffn_ld) = sems("mask_ld", "ctx_ld", "ffn_ld")
        exp_ld = sems("expert_ld0", "expert_ld1")
        (half_set, coef_neg, nmask_done, nb_copied, dve_chain, var_ready, std_ready, x_written,
         xn_done) = sems("half_set", "coef_neg", "nmask_done", "nb_copied", "dve_chain", "var_ready",
                         "std_ready", "x_written", "xn_done")
        (scores, scored, exped, turned, turn_copied, on_done, rinv_done, mm, mm_copied,
         relu_done, term_done) = sems("scores", "scored", "exped", "turned", "turn_copied",
                                      "on_done", "rinv_done", "mm", "mm_copied", "relu_done", "term_done")
        (sa_qkv, sa_rope, sa_turned, sa_qkT, sa_qm, sa_scores, sa_scored, sa_exp, sa_pT, sa_pTc,
         sa_pv, sa_on, sa_oT, sa_oTc, sa_y) = sems(
            "sa_qkv", "sa_rope", "sa_turned", "sa_qkT", "sa_qm", "sa_scores", "sa_scored", "sa_exp", "sa_pT",
            "sa_pTc", "sa_pv", "sa_on", "sa_oT", "sa_oTc", "sa_y")
        (mo_x, mo_xT, mo_xTc, mo_sc, mo_scc, mo_max, mo_e, mo_w, mo_wT, mo_wTc, mo_h, mo_sil, mo_g, mo_y,
         mo_acc, out_ready) = sems(
            "mo_x", "mo_xT", "mo_xTc", "mo_sc", "mo_scc", "mo_max", "mo_e", "mo_w", "mo_wT", "mo_wTc", "mo_h",
            "mo_sil", "mo_g", "mo_y", "mo_acc", "out_ready")

        sa_x = sb("sa_x", [P, FT, D])
        sa_xT = sb("sa_xT", [P, S])
        cos = sb("cos", [P, FT, 2 * D])
        sin = sb("sin", [P, FT, 2 * D])
        wqkvT = sb("wqkvT", [P, 3 * D])
        woT = sb("woT", [P, D])
        hmask = sb("hmask", [P, SH])
        cmask = sb("cmask", [P, 3 * P])
        flatT = probT[:, :, :, :].rearrange("p a b c -> p (a b c)")
        flatV = val[:, :, :, :].rearrange("p a b c -> p (a b c)")
        qkr = flatT[:, 0:512].rearrange("p (a b) -> p a b", a=2)
        rot1 = flatT[:, 512:1024].rearrange("p (a b) -> p a b", a=2)
        rot2 = flatT[:, 1024:1536].rearrange("p (a b) -> p a b", a=2)
        v_sa = flatT[:, 1536:1792].rearrange("p (a b) -> p a b", a=2)
        qkT = flatT[:, 1792:2304].rearrange("p (a b) -> p a b", a=2)
        o_sa = flatT[:, 2304:2560].rearrange("p (a b) -> p a b", a=2)
        oT_sa = flatT[:, 2560:2816]
        qm = flatV[:, 0:1024].rearrange("p (a b) -> p a b", a=GH)
        flatP = prob[:, :, :].rearrange("p a b -> p (a b)")
        s_sa = flatP[:, 0:1536].rearrange("p (a b) -> p a b", a=GH)
        pT_sa = flatP[:, 1536:3072].rearrange("p (a b) -> p a b", a=GH)
        nm_sa = sb("nm_sa", [P, 2, GH])
        rs_sa = sb("rs_sa", [P, 2, GH])
        ri_sa = sb("ri_sa", [P, 2, GH])

        flatR = relu[:, :, :, :].rearrange("p a b c -> p (a b c)")
        flatD = dist[:, :, :, :].rearrange("p a b c -> p (a b c)")
        x2T = flatR[:, 0:1024]
        sil = flatR[:, 1024:3072].rearrange("p (a b) -> p a b", a=2)
        gat = flatR[:, 3072:5120].rearrange("p (a b) -> p a b", a=2)
        x2 = flatD[:, 0:1024].rearrange("p (a b) -> p a b", a=TILES)
        acc = flatD[:, 1024:2048].rearrange("p (a b) -> p a b", a=TILES)
        wexp = flatD[:, 2048:3584].rearrange("p (a b) -> p a b", a=2)
        wgT = flatD[:, 3584:3592]
        yout = flatD[:, 4096:5120].rearrange("p (a b) -> p a b", a=TILES)
        flatN = nb_next[:, :, :].rearrange("p a b -> p (a b)")
        flatC = nb_cur[:, :, :].rearrange("p a b -> p (a b)")
        sc8 = flatN[0:E, 0:1024]
        work = flatN[0:E, 1024:2048]
        ex8 = flatN[0:E, 2048:3072]
        keep = flatC[0:E, 0:1024]
        w8 = flatC[0:E, 1024:2048]
        top8 = sb("top8", [E, 8])
        sm8 = sb("sm8", [E, 4])
        tick = sb("tick", [P, 1])
        wT = sb("wT", [P, TILES, E])

        x_tiles = d["x"].rearrange("b (t p) d -> b p t d", p=P)
        f_tiles = d["fside"].rearrange("b (t p) k -> b p t k", p=P)

        def tiles_of(g):
            return range(4 * g, min(4 * g + 4, TT))

        def rows_of(t):
            return P if t < TT - 1 else LAST

        block = ctx.enter_context(nc.Block())

        def apart(eng):
            eng.sem_inc(carried, 1)

        @block.sync
        def _(sp):
            sp.sem_inc(scored, 2)
            sp.sem_inc(turned, 2 * TG)
            sp.sem_inc(turn_copied, 2)
            sp.sem_inc(on_done, 4)
            sp.sem_inc(mm_copied, 2)
            sp.sem_inc(term_done, 2)
            for dst, name in ((ident, "ident"), (wqkvT, "wqkvT"), (woT, "woT"), (hmask, "hmask"),
                              (cmask, "cmask"), (cos, "cos"), (sin, "sin")):
                sp.dma_start(dst[:], d[name]).then_inc(const_ld, 16)
            for dst, name in ((coef[:, 0], "wth"), (coef[:, 1], "bth"), (negc[:], "wto"), (nbto[:], "bto")):
                sp.dma_start(dst, d[name].to_broadcast(dst.shape)).then_inc(coef_ld, 16)
            sp.dma_start(maskb[:], d["mask"][0].to_broadcast([P, T])).then_inc(mask_ld, 16)
            sp.dma_start(dist[:, 0], f_tiles[0]).then_inc(dist_ld, 16)
            sp.wait_ge(nmask_done, 1)
            sp.dma_start(maskb[:], d["mask"][1].to_broadcast([P, T])).then_inc(mask_ld, 16)
            with sp.Fori(0, B) as b:
                sp.dma_start(sa_xT[:], d["xT"][b]).then_inc(xT_ld, 16)
                sp.dma_start(sa_x[:], x_tiles[b]).then_inc(x_ld, 16)
                sp.wait_ge(x_written, b + 1)
                apart(sp)
            sp.wait_ge(dist_ld, 16)
            sp.dma_start(dist[:, 1], f_tiles[1]).then_inc(dist_ld, 16)
            for p in range(2):
                sp.dma_start(wqkv[:, p], d["wqkv"][p]).then_inc(w_ld[p], 16)
                sp.dma_start(wo[:, p], d["wo"][p]).then_inc(wo_ld[p], 16)

            with sp.Fori(0, STEPS) as s:
                sp.wait_ge(x_written, B + s)
                sp.dma_start(ctxT[:], d["ctxT"][s % B]).then_inc(ctx_ld, 16)
                layer = s // B
                for dst, name in ((wf1, "wf1"), (wf2, "wf2"), (bf1, "bf1")):
                    sp.dma_start(dst[:], d[name][layer]).then_inc(ffn_ld, 16)
                sp.dma_start(bf2[:], d["bf2"][layer].to_broadcast([P, D])).then_inc(ffn_ld, 16)
                sp.wait_ge(dist_ld, 16 * (s + 2))
                sp.wait_ge(relu_done, HID * (s + 1))
                sp.dma_start(dist[:, s % 2], f_tiles[(s + 2) % B]).then_inc(dist_ld, 16)
                sp.wait_ge(nmask_done, s + 2)
                sp.dma_start(maskb[:], d["mask"][(s + 2) % B].to_broadcast([P, T])).then_inc(mask_ld, 16)

                def load_wo(p):
                    y = (BASE_TAIL + TAIL.index("Y0") if p == PAIRS - 1 else
                         BASE_MIDDLE + PER_PAIR * (p + 1) + flat(FINAL if p == PAIRS - 2 else MIDDLE).index("Y"))
                    sp.wait_ge(mm, s * TASKS + y + 1)
                    sp.dma_start(wo[:, p % 2], d["wo"][weights_row(s, p + 2)]).then_inc(wo_ld[p % 2], 16)

                for p in range(PAIRS):
                    v3 = BASE_FIRST if p == 0 else BASE_MIDDLE + PER_PAIR * p
                    sp.wait_ge(mm, s * TASKS + v3 + 1)
                    sp.dma_start(wqkv[:, p % 2], d["wqkv"][weights_row(s, p + 2)]).then_inc(w_ld[p % 2], 16)
                    if p >= 1:
                        load_wo(p - 1)
                load_wo(PAIRS - 1)

            sp.wait_ge(mo_x, 1)
            sp.dma_start(wgT, d["wgT"]).then_inc(gate_ld, 16)
            for e in range(2):
                sp.dma_start(wexp[:, e], d["wexp"][e]).then_inc(exp_ld[e], 16)
            for e in range(2, E):
                sp.wait_ge(mo_y, 2 * (e - 1))
                sp.dma_start(wexp[:, e % 2], d["wexp"][e]).then_inc(exp_ld[e % 2], 16)
            sp.wait_ge(out_ready, 1)
            sp.dma_start(d["out"].rearrange("b (t p) d -> p (b t) d", p=P), yout).then_inc(out_st, 16)
            sp.wait_ge(out_st, 16)

        @block.gpsimd
        def _(pool):
            nc.gpsimd.memset(half[:], 0.5).then_inc(half_set, 1)
            pool.wait_ge(half_set, 1)

            def root(n, width):
                pool.wait_ge(var_ready, n + 1)
                nc.gpsimd.tensor_tensor(sd[:, 0:width], vv[:, 0:width], half[:, 0:width], ALU.pow
                                        ).then_inc(std_ready, 1)

            with pool.Fori(0, B + NORMS * STEPS) as n:
                root(n, FT)
            for n in range(3):
                root(B + NORMS * STEPS + n, TILES)

        @block.tensor
        def _(pe):
            mat = nc.tensor.matmul

            def turn(out, in_, k=P):
                return nc.tensor.transpose(out, in_, ident[0:k, 0:k])

            pe.wait_ge(const_ld, 16 * 7)
            with pe.Fori(0, B) as b:
                pe.wait_ge(xT_ld, 16 * (b + 1))
                for ft in range(FT):
                    mat(psum[:, 6 + ft, 0:3 * D], sa_xT[:, ft * P:(ft + 1) * P], wqkvT[:], start=True, stop=True
                        ).then_inc(sa_qkv, 1)
                pe.wait_ge(sa_rope, b + 1)
                for a in range(2):
                    for ft in range(FT):
                        last = turn(psum[:, 6, (2 * a + ft) * P:(2 * a + ft + 1) * P], qkr[:, ft, a * D:(a + 1) * D])
                last.then_inc(sa_turned, 1)
                with pe.Fori(0, SG) as g:
                    group = b * SG + g
                    for h in range(GH):
                        pe.wait_ge(sa_qm, GH * group + h + 1)
                        mat(psum[:, h, 0:P], qm[:, h, 0:P], qkT[:, 1, 0:P], start=True, stop=True)
                        mat(psum[:, h, P:3 * P], qm[:, h, P:2 * P], qkT[:, 1, :], start=True, stop=True
                            ).then_inc(sa_scores, 1)
                    for h in range(GH):
                        pe.wait_ge(sa_exp, GH * group + h + 1)
                        if h >= 2:
                            pe.wait_ge(sa_pTc, GH * group + h - 1)
                        for c in range(3):
                            last = turn(psum[:, 4 + h % 2, c * P:(c + 1) * P], s_sa[:, h, c * P:(c + 1) * P])
                        last.then_inc(sa_pT, 1)
                    pe.wait_ge(sa_pTc, GH * group + GH)
                    for h in range(GH):
                        vs = [v_sa[:, ft, bass.ds(g * (GH * SHD) + h * SHD, SHD)] for ft in range(FT)]
                        o = [psum[:, 7, (a * GH + h) * SHD:(a * GH + h + 1) * SHD] for a in range(2)]
                        mat(o[0], pT_sa[:, h, 0:P], vs[0], start=True, stop=True)
                        mat(o[1], pT_sa[:, h, P:2 * P], vs[0], start=True, stop=False)
                        last = mat(o[1], pT_sa[:, h, 2 * P:3 * P], vs[1], start=False, stop=True)
                    last.then_inc(sa_pv, 1)
                pe.wait_ge(sa_on, (b + 1) * SG)
                for ft in range(FT):
                    last = turn(psum[:, 6, ft * P:(ft + 1) * P], o_sa[:, ft, :])
                last.then_inc(sa_oT, 1)
                pe.wait_ge(sa_oTc, b + 1)
                for ft in range(FT):
                    last = mat(psum[:, 7, ft * P:(ft + 1) * P], oT_sa[:, ft * P:(ft + 1) * P], woT[:],
                               start=True, stop=True)
                last.then_inc(sa_y, 1)

            def task(kind, s, local, bank, p, parity):
                n, ps = s * TASKS + local, psum[:, bank, :]
                if kind == "XN1":
                    pe.wait_ge(mm_copied, n + 2)
                    pe.wait_ge(xn_done, NORMS * s + 1)
                elif kind in ("OT", "Y", "V0", "V1", "V2", "V3", "Q", "H1"):
                    pe.wait_ge(mm_copied, n + 1)
                else:
                    pe.wait_ge(mm_copied, n + 2)
                if kind[0] == "X":
                    if kind == "XN2":
                        pe.wait_ge(xn_done, NORMS * s + 2)
                    for ft in range(FT):
                        last = turn(ps[:, ft * P:(ft + 1) * P], xn[:, ft, :])
                elif kind in ("Q", "Q0"):
                    pe.wait_ge(w_ld[parity], 16 * (s * (PAIRS // 2) + p // 2 + 1))
                    last = mat(ps[:, 0:S], wqkv[:, parity, 0, :], xnT[:], start=True, stop=True)
                elif kind == "QK":
                    last = mat(ps, wqkv[:, parity, 1, :], q_sb[:, :, :].rearrange("p h c -> p (h c)"),
                               start=True, stop=True)
                elif kind[0] == "V":
                    for i, t in enumerate(tiles_of(int(kind[1]))):
                        m = rows_of(t)
                        last = mat(ps[0:m, i * P:(i + 1) * P], ctxT[:, t * P:t * P + m], wqkv[:, parity, 2, :],
                                   start=True, stop=True)
                elif kind == "OT":
                    pe.wait_ge(on_done, 4 + s * UNITS + 4 * (p + 1))
                    for ft in range(FT):
                        last = turn(ps[:, ft * P:(ft + 1) * P], On[:, parity, ft, :])
                elif kind in ("Y", "Y0"):
                    pe.wait_ge(wo_ld[parity], 16 * (s * (PAIRS // 2) + p // 2 + 1))
                    for ft in range(FT):
                        last = mat(ps[:, ft * P:(ft + 1) * P], OT[:, ft * P:(ft + 1) * P], wo[:, parity, :],
                                   start=True, stop=True)
                elif kind[0] == "H":
                    if kind == "H0":
                        pe.wait_ge(ffn_ld, 64 * (s + 1))
                    for i in range(2):
                        f = 2 * int(kind[1]) + i
                        last = mat(ps[:, i * S:(i + 1) * S], wf1[:, f * P:(f + 1) * P], xnT[:],
                                   start=True, stop=True)
                else:
                    for ft in range(FT):
                        for f in range(FB):
                            last = mat(ps[:, ft * P:(ft + 1) * P], hT[:, f, ft * P:(ft + 1) * P], wf2[:, f, :],
                                       start=(f == 0), stop=(f == FB - 1))
                last.then_inc(mm, 1)

            def unit_scores(s, u, k, parity, qk_task):
                n = s * UNITS + u
                if k == 0:
                    pe.wait_ge(mm_copied, s * TASKS + qk_task + 3)
                for c, (lo, hi) in enumerate(((0, CUT), (CUT, T))):
                    pe.wait_ge(scored, 2 * n + c + 1)
                    for i, a in enumerate(range(lo, hi, 512)):
                        z = min(a + 512, hi)
                        last = mat(psum[:, 2 * c + i, 0:z - a],
                                   qk_sb[:, parity, k // 2, (k % 2) * P:(k % 2 + 1) * P], ctxT[:, a:z],
                                   start=True, stop=True)
                    last.then_inc(scores, 1)

            def unit_turn(s, u, k, groups):
                n = s * UNITS + u
                for g in groups:
                    if g == 0:
                        pe.wait_ge(exped, n + 1)
                    pe.wait_ge(turn_copied, TG * n + g + 1)
                    for i, t in enumerate(tiles_of(g)):
                        m = rows_of(t)
                        last = turn(psum[0:m, 4 + g % 2, i * P:(i + 1) * P], prob[:, k % 2, t * P:t * P + m])
                    last.then_inc(turned, 1)

            def unit_pv(s, u, k, local, bank, parity, v3_task):
                n = s * UNITS + u
                pe.wait_ge(turn_copied, TG * (n + 1) + 2)
                pe.wait_ge(mm_copied, s * TASKS + local + 1)
                if k == 0:
                    pe.wait_ge(mm_copied, s * TASKS + v3_task + 3)
                for t in range(TT):
                    m, h = rows_of(t), k // 2
                    last = mat(psum[:, bank, 0:HD], probT[0:m, k % 2, t, :],
                               val[0:m, parity, t, h * HD:(h + 1) * HD], start=(t == 0), stop=(t == TT - 1))
                last.then_inc(mm, 1)

            def pair(s, p, parity, kind, base, qk_task):
                off = 0
                for k in range(4):
                    u = 4 * p + k
                    unit_scores(s, u, k, parity, qk_task)
                    for i, name in enumerate(kind[k]):
                        if i == 1 and (kind is not FIRST or k >= 1):
                            unit_turn(s, u - 1, (k - 1) % 4, (0, 1))
                        if name == "PV":
                            unit_pv(s, u - 2, (k - 2) % 4, base + off, 6 + off % 2,
                                    parity if k >= 2 else 1 - parity, base)
                        elif name:
                            task(name, s, base + off, 6 + off % 2, *pair_of(name, p, parity))
                        off += 1 if name else 0
                        if i == 1 and (kind is not FIRST or k >= 1):
                            unit_turn(s, u - 1, (k - 1) % 4, (2, 3))

            with pe.Fori(0, STEPS) as s:
                pe.wait_ge(ctx_ld, 16 * (s + 1))
                for i, name in enumerate(START):
                    task(name, s, i, 6 + i % 2, 0, 0)
                pairs_of(s, pair, pe.Fori)
                unit_turn(s, UNITS - 1, 3, range(TG))
                for i, name in enumerate(TAIL):
                    at = (BASE_TAIL + i, 6 + (BASE_TAIL + i) % 2)
                    if name == "PV":
                        unit_pv(s, UNITS - 2 + i, 2 + i, *at, 1, None)
                    else:
                        task(name, s, *at, PAIRS - 1, 1)

            pe.wait_ge(mo_x, 1)
            for t in range(TILES):
                last = turn(psum[:, t // 4, t % 4 * P:(t % 4 + 1) * P], x2[:, t, :])
            last.then_inc(mo_xT, 1)
            pe.wait_ge(mo_xTc, 1)
            pe.wait_ge(gate_ld, 16)
            for c in range(2):
                last = mat(psum[0:E, 2 + c, :], wgT, x2T[:, c * 512:(c + 1) * 512], start=True, stop=True)
            last.then_inc(mo_sc, 1)
            for e in range(E):
                if e == 0:
                    pe.wait_ge(mo_scc, 1)
                pe.wait_ge(exp_ld[e % 2], 16 * (e // 2 + 1))
                for hh in range(2):
                    for c in range(2):
                        i = 4 * e + 2 * hh + c
                        if i >= 2:
                            pe.wait_ge(mo_g, i - 1)
                        for a in range(2):
                            last = mat(psum[:, 2 * (i % 2) + a, :],
                                       wexp[:, e % 2, a * EH + hh * P:a * EH + (hh + 1) * P],
                                       x2T[:, c * 512:(c + 1) * 512], start=True, stop=True)
                        last.then_inc(mo_h, 1)
                if e == 0:
                    pe.wait_ge(mo_w, 1)
                    for t in range(TILES):
                        last = turn(psum[:, 6, t * E:(t + 1) * E], w8[:, t * P:(t + 1) * P], E)
                    last.then_inc(mo_wT, 1)
                pe.wait_ge(mo_g, 4 * (e + 1))
                for c in range(2):
                    if e >= 1:
                        pe.wait_ge(mo_acc, 2 * (e - 1) + c + 1)
                    for i in range(4):
                        t = 4 * c + i
                        for hh in range(2):
                            last = mat(psum[:, 4 + c, i * P:(i + 1) * P], gat[:, hh, t * P:(t + 1) * P],
                                       wexp[:, e % 2, 2 * EH + hh * P:2 * EH + (hh + 1) * P],
                                       start=(hh == 0), stop=(hh == 1))
                    last.then_inc(mo_y, 1)

        @block.scalar
        def _(act):
            fun = nc.scalar.activation

            def bias_relu(n, buf, slot, first):
                act.wait_ge(term_done, n + 1)
                fun(relu[:, buf], slot, ACT.Relu, bias=coef[:, 1, bass.ds(n, 1)],
                    scale=coef[:, 0, bass.ds(n, 1)]).then_inc(relu_done, 1)

            act.wait_ge(coef_ld, 16 * 4)
            act.wait_ge(dist_ld, 16)
            with act.Fori(0, B * SG) as group:
                for h in range(GH):
                    for a in range(2):
                        act.wait_ge(sa_scored, 2 * GH * group + 2 * h + a + 1)
                        part = s_sa[:, h, 0:P] if a == 0 else s_sa[:, h, P:3 * P]
                        last = fun(part, part, ACT.Exp, scale=-1.0, bias=nm_sa[:, a, h:h + 1],
                                   accum_out=rs_sa[:, a, h:h + 1])
                    last.then_inc(sa_exp, 1)
                for i in range(2):
                    bias_relu(2 * group + i, i, dist[:, 0], False)
                for h in range(GH):
                    act.wait_ge(sa_pT, GH * group + h + 1)
                    fun(pT_sa[:, h, :], psum[:, 4 + h % 2, 0:3 * P], ACT.Copy).then_inc(sa_pTc, 1)

            def unit_exp(s, u, k):
                n = s * UNITS + u
                act.wait_ge(scored, 2 * n + 4)
                fun(prob[:, k % 2, :], prob[:, k % 2, :], ACT.Exp, scale=-1.0, bias=nm[:, k:k + 1],
                    accum_out=rsum[:, k:k + 1]).then_inc(exped, 1)

            def unit_copy(s, u, k):
                n = s * UNITS + u
                for g in range(TG):
                    act.wait_ge(turned, TG * (n + 2) + g + 1)
                    if g == 0:
                        act.wait_ge(on_done, n + 3)
                    ts = tiles_of(g)
                    m = rows_of(ts[-1])
                    fun(probT[0:m, k % 2, ts[0]:ts[-1] + 1, :],
                        psum[0:m, 4 + g % 2, 0:len(ts) * P].rearrange("p (t q) -> p t q", q=P), ACT.Copy
                        ).then_inc(turn_copied, 1)

            def pair(s, p, parity, kind, base, qk_task):
                for k in range(4):
                    u = 4 * p + k
                    go = kind is not FIRST or k >= 1
                    if go:
                        unit_exp(s, u - 1, (k - 1) % 4)
                    bias_relu((s + 1) * HID + u, k % 2, dist[:, (s + 1) % 2], False)
                    if go:
                        unit_copy(s, u - 1, (k - 1) % 4)

            with act.Fori(0, STEPS) as s:
                act.wait_ge(dist_ld, 16 * (s + 2))
                pairs_of(s, pair, act.Fori)
                unit_exp(s, UNITS - 1, 3)
                unit_copy(s, UNITS - 1, 3)

            act.wait_ge(mo_max, 1)
            fun(ex8, sc8, ACT.Exp, bias=sm8[:, 0:1]).then_inc(mo_e, 1)
            for i in range(4 * E):
                act.wait_ge(mo_h, i + 1)
                if i >= 2:
                    act.wait_ge(mo_g, i - 1)
                fun(sil[:, i % 2, 0:512], psum[:, 2 * (i % 2), :], ACT.Silu).then_inc(mo_sil, 1)

        @block.vector
        def _(dve):
            v = nc.vector
            chain = {"base": 0, "n": 0}

            def link(ins):
                chain["n"] += 1
                ins.then_inc(dve_chain, 1)
                dve.wait_ge(dve_chain, chain["base"] + chain["n"])

            def norm(n, src, width, before, after, out, done):
                for t in range(width):
                    last = v.bn_stats(bn[:, t, :], src(t))
                link(last)
                apart(dve)
                for t in range(width):
                    last = v.bn_aggr(mv[:, t, :], bn[:, t, :])
                link(last)
                v.tensor_scalar(vv[:, 0:width], mv[:, 0:width, 1], before, None, ALU.add).then_inc(var_ready, 1)
                dve.wait_ge(std_ready, n + 1)
                link(v.tensor_scalar(rs[:, 0:width], sd[:, 0:width], after, None, ALU.add))
                link(v.reciprocal(rs[:, 0:width], rs[:, 0:width]))
                for t in range(width):
                    last = v.tensor_scalar(out(t), src(t), mv[:, t, 0:1], rs[:, t:t + 1], ALU.subtract, ALU.mult)
                last.then_inc(done, 1)

            def bias_term(n, buf, first):
                dve.wait_ge(relu_done, n + 1)
                dve.wait_ge(term_done, n + 2)
                for ft in range(FT):
                    start = nmask[:, :] if first else nb_next[:, ft, :]
                    last = v.scalar_tensor_tensor(out=nb_next[:, ft, :], in0=relu[:, buf, ft, :],
                                                  scalar=negc[:, bass.ds(n, 1)], in1=start,
                                                  op0=ALU.mult, op1=ALU.add)
                last.then_inc(term_done, 1)

            v.memset(q_sb[:], 0.0)
            dve.wait_ge(coef_ld, 16 * 4)
            v.tensor_scalar(negc[:], negc[:], -1.0, None, ALU.mult)
            link(v.tensor_scalar(nbto[:], nbto[:], -1.0, None, ALU.mult))
            dve.wait_ge(mask_ld, 16)
            v.tensor_scalar(nmask[:], maskb[:], -1.0, nbto[:, 0:1], ALU.mult, ALU.add).then_inc(nmask_done, 1)
            dve.wait_ge(nmask_done, 1)
            for ft in range(FT):
                last = v.tensor_copy(nb_next[:, ft, :], nmask[:])
            link(last)
            dve.wait_ge(const_ld, 16 * 7)
            setup = chain["n"]

            with dve.Fori(0, B) as b:
                chain["base"], chain["n"] = setup + b * CHAIN_SA, 0
                dve.wait_ge(sa_qkv, FT * (b + 1))
                for ft in range(FT):
                    ps = psum[:, 6 + ft, 0:2 * D]
                    v.tensor_tensor(rot1[:, ft, :], ps, cos[:, ft, :], ALU.mult)
                    two = [x.rearrange("p (i two) -> p i two", two=2) for x in (rot2[:, ft, :], ps, sin[:, ft, :])]
                    for a in range(2):
                        last = v.tensor_tensor(two[0][:, :, a], two[1][:, :, 1 - a], two[2][:, :, a], ALU.mult)
                    v.tensor_copy(v_sa[:, ft, :], psum[:, 6 + ft, 2 * D:3 * D])
                link(last)
                v.tensor_tensor(qkr, rot1, rot2, ALU.add).then_inc(sa_rope, 1)
                dve.wait_ge(sa_turned, b + 1)
                link(v.tensor_copy(qkT, psum[:, 6, :].rearrange("p (a c) -> p a c", a=2)))
                apart(dve)
                with dve.Fori(0, SG) as g:
                    group = b * SG + g
                    for h in range(GH):
                        v.tensor_scalar(qm[:, h, :], qkT[:, 0, :], hmask[:, bass.ds(g * GH + h, 1)], None, ALU.mult
                                        ).then_inc(sa_qm, 1)
                    for h in range(GH):
                        dve.wait_ge(sa_scores, GH * group + h + 1)
                        for a, (lo, hi) in enumerate(((0, P), (P, 3 * P))):
                            apart(dve)
                            v.tensor_tensor_reduce(out=s_sa[:, h, lo:hi], in0=psum[:, h, lo:hi],
                                                   in1=cmask[:, lo:hi], scale=1.0, scalar=BIG, op0=ALU.add,
                                                   op1=ALU.min, accum_out=nm_sa[:, a, h:h + 1]).then_inc(sa_scored, 1)
                    for i in range(2):
                        bias_term(2 * group + i, i, False)
                    dve.wait_ge(sa_pv, group + 1)
                    v.reciprocal(ri_sa[:], rs_sa[:]).then_inc(sa_ri, 1)
                    dve.wait_ge(sa_ri, group + 1)
                    v.tensor_tensor(o_sa[:, :, bass.ds(g * GH * SHD, GH * SHD)].rearrange("p a (h c) -> p a h c", c=SHD),
                                    psum[:, 7, 0:2 * GH * SHD].rearrange("p (a h c) -> p a h c", a=2, c=SHD),
                                    ri_sa[:].rearrange("p a (h o) -> p a h o", o=1).to_broadcast([P, 2, GH, SHD]),
                                    ALU.mult).then_inc(sa_on, 1)
                dve.wait_ge(sa_oT, b + 1)
                v.tensor_copy(oT_sa, psum[:, 6, 0:S]).then_inc(sa_oTc, 1)
                dve.wait_ge(sa_y, b + 1)
                dve.wait_ge(x_ld, 16 * (b + 1))
                link(v.tensor_tensor(xcur[:], sa_x[:], psum[:, 7, 0:S].rearrange("p (a c) -> p a c", a=2), ALU.add))
                norm(b, lambda t: xcur[:, t, :], FT, 1e-5, 0.0, lambda t: xs[:, b, t, :], x_written)
                chain_sa = chain["n"]
            assert chain_sa == CHAIN_SA, chain_sa
            after_sa = setup + B * CHAIN_SA

            def copy(kind, s, local, bank, p, parity):
                n, ps = s * TASKS + local, psum[:, bank, :]
                dve.wait_ge(mm, n + 1)
                if kind[0] == "X":
                    last = v.tensor_copy(xnT[:], ps[:, 0:S])
                elif kind in ("Q", "Q0"):
                    for h in range(2):
                        k = slice(h * HD, (h + 1) * HD)
                        last = v.tensor_scalar(q_sb[k, h, :], ps[k, 0:S], -float(HD) ** -0.5, None, ALU.mult)
                elif kind == "QK":
                    last = v.tensor_copy(qk_sb[:, parity], ps.rearrange("p (h c) -> p h c", h=2))
                elif kind[0] == "V":
                    ts = tiles_of(int(kind[1]))
                    m = rows_of(ts[-1])
                    last = v.tensor_copy(val[0:m, parity, ts[0]:ts[-1] + 1, :],
                                         ps[0:m, 0:len(ts) * P].rearrange("p (t c) -> p t c", c=P))
                elif kind == "OT":
                    last = v.tensor_copy(OT[:], ps[:, 0:S])
                elif kind in ("Y", "Y0"):
                    last = v.tensor_tensor(xcur[:], xcur[:], ps[:, 0:S].rearrange("p (a c) -> p a c", a=2), ALU.add)
                elif kind[0] == "H":
                    for i in range(2):
                        f = 2 * int(kind[1]) + i
                        last = v.tensor_scalar(hT[:, f, :], ps[:, i * S:(i + 1) * S], bf1[:, f:f + 1], 0.0,
                                               ALU.add, ALU.max)
                last.then_inc(mm_copied, 1)

            def unit_add(s, u, k):
                n = s * UNITS + u
                dve.wait_ge(turned, TG * (n + 1))
                for c, (lo, hi) in enumerate(((0, CUT), (CUT, T))):
                    dve.wait_ge(scores, 2 * n + c + 1)
                    if c == 1:
                        dve.wait_ge(scored, 2 * n + 3)
                    apart(dve)
                    v.tensor_tensor_reduce(
                        out=prob[:, k % 2, lo:hi],
                        in0=psum[:, 2 * c:2 * c + 2, :].rearrange("p a b -> p (a b)")[:, 0:hi - lo],
                        in1=nb_cur[:, k % 2, lo:hi], scale=1.0, scalar=BIG if c == 0 else nmA[:, k:k + 1],
                        op0=ALU.add, op1=ALU.min, accum_out=(nmA if c == 0 else nm)[:, k:k + 1]).then_inc(scored, 1)

            def unit_norm(s, u, k, local, bank, parity):
                n = s * UNITS + u
                dve.wait_ge(mm, s * TASKS + local + 1)
                v.reciprocal(rinv[:, k:k + 1], rsum[:, k:k + 1]).then_inc(rinv_done, 1)
                dve.wait_ge(rinv_done, n + 1)
                v.tensor_scalar(On[:, parity, k % 2, (k // 2) * HD:(k // 2 + 1) * HD],
                                psum[:, bank, 0:HD], rinv[:, k:k + 1], None, ALU.mult
                                ).then_inc(mm_copied, 1)
                v.memset(tick[:], 0.0).then_inc(on_done, 1)

            def pair(s, p, parity, kind, base, qk_task):
                off = 0
                for k in range(4):
                    u = 4 * p + k
                    unit_add(s, u, k)
                    for name in kind[k]:
                        if name == "PV":
                            unit_norm(s, u - 2, (k - 2) % 4, base + off, 6 + off % 2,
                                      parity if k >= 2 else 1 - parity)
                        elif name:
                            copy(name, s, base + off, 6 + off % 2, *pair_of(name, p, parity))
                        off += 1 if name else 0
                    bias_term((s + 1) * HID + u, k % 2, kind is FIRST and k == 0)

            with dve.Fori(0, STEPS) as s:
                chain["base"], chain["n"] = after_sa + s * CHAIN_STEP, 0
                dve.wait_ge(x_written, s + 1)
                norm(B + NORMS * s, lambda t: xs[:, s, t, :], FT, 0.0, 1e-6, lambda t: xn[:, t, :], xn_done)
                v.tensor_copy(xcur[:], xs[:, s])
                dve.wait_ge(term_done, HID * (s + 1) + 2)
                v.tensor_copy(nb_cur[:], nb_next[:])
                dve.wait_ge(mask_ld, 16 * (s + 2))
                v.tensor_scalar(nmask[:], maskb[:], -1.0, nbto[:, bass.ds(s + 1, 1)], ALU.mult, ALU.add
                                ).then_inc(nmask_done, 1)
                dve.wait_ge(nmask_done, s + 2)
                for i, name in enumerate(START):
                    copy(name, s, i, 6 + i % 2, 0, 0)
                pairs_of(s, pair, dve.Fori)
                for i, name in enumerate(TAIL):
                    n, bank = s * TASKS + BASE_TAIL + i, 6 + (BASE_TAIL + i) % 2
                    if name == "XN2":
                        dve.wait_ge(mm_copied, n + 2)
                        norm(B + NORMS * s + 1, lambda t: xcur[:, t, :], FT, 0.0, 1e-6, lambda t: xn[:, t, :],
                             xn_done)
                        dve.wait_ge(xn_done, NORMS * (s + 1))
                        dve.wait_ge(ffn_ld, 64 * (s + 1))
                        link(v.tensor_tensor(xcur[:], xcur[:],
                                             bf2[:].rearrange("p (o c) -> p o c", o=1).to_broadcast([P, FT, D]),
                                             ALU.add))
                    if name == "Y2":
                        dve.wait_ge(mm, n + 1)
                        v.tensor_tensor(xs[:, s + B], xcur[:],
                                        psum[:, bank, 0:S].rearrange("p (a c) -> p a c", a=2), ALU.add
                                        ).then_inc(mm_copied, 1)
                        v.memset(tick[:], 0.0).then_inc(x_written, 1)
                    elif name == "PV":
                        unit_norm(s, UNITS - 2 + i, 2 + i, BASE_TAIL + i, bank, 1)
                    else:
                        copy(name, s, BASE_TAIL + i, bank, PAIRS - 1, 1)
                chain_step = chain["n"]
            assert chain_step == CHAIN_STEP, chain_step
            chain["base"], chain["n"] = after_sa + STEPS * CHAIN_STEP, 0

            first = B + NORMS * STEPS
            dve.wait_ge(x_written, B + STEPS)
            dve.wait_ge(dist_ld, 16 * (STEPS + 2))
            dve.wait_ge(relu_done, HID * (STEPS + 1))
            norm(first, lambda t: xs[:, STEPS + t // FT, t % FT, :], TILES, 0.0, 1e-6, lambda t: x2[:, t, :], mo_n)
            dve.wait_ge(mo_n, 1)
            link(v.tensor_tensor(acc.rearrange("p t d -> p (t d)"), x2.rearrange("p t d -> p (t d)"),
                                 xs[:, 0:B].rearrange("p b t d -> p (b t d)"), ALU.add))
            norm(first + 1, lambda t: acc[:, t, :], TILES, 1e-5, 0.0, lambda t: x2[:, t, :], mo_x)
            dve.wait_ge(mo_x, 1)
            link(v.tensor_copy(acc, x2))

            dve.wait_ge(mo_xT, 1)
            v.tensor_copy(x2T, psum[:, 0:2, :].rearrange("p a b -> p (a b)")).then_inc(mo_xTc, 1)
            dve.wait_ge(mo_sc, 1)
            v.tensor_copy(sc8, psum[0:E, 2:4, :].rearrange("p a b -> p (a b)"))
            link(v.tensor_copy(work, psum[0:E, 2:4, :].rearrange("p a b -> p (a b)")))
            for r in range(CAP // 8):
                link(v.max(top8[:], work))
                if r == 0:
                    v.tensor_scalar(sm8[:, 0:1], top8[:, 0:1], -1.0, None, ALU.mult).then_inc(mo_max, 1)
                    v.memset(tick[:], 0.0).then_inc(mo_scc, 1)
                link(v.match_replace(out=work, in_to_replace=top8[:], in_values=work, imm_value=-BIG))
            link(v.tensor_tensor(keep, work, sc8, ALU.not_equal))
            dve.wait_ge(mo_e, 1)
            link(v.tensor_tensor_reduce(out=w8, in0=ex8, in1=keep, scale=1.0, scalar=0.0, op0=ALU.mult,
                                        op1=ALU.add, accum_out=sm8[:, 1:2]))
            link(v.reciprocal(sm8[:, 2:3], sm8[:, 1:2]))
            v.tensor_scalar(w8, w8, sm8[:, 2:3], None, ALU.mult).then_inc(mo_w, 1)

            def gate(i):
                hh, c = i // 2 % 2, i % 2
                dve.wait_ge(mo_sil, i + 1)
                if i >= 4 and i % 4 == 0:
                    dve.wait_ge(mo_y, 2 * (i // 4))
                v.tensor_tensor(gat[:, hh, c * 512:(c + 1) * 512], sil[:, i % 2, 0:512],
                                psum[:, 2 * (i % 2) + 1, :], ALU.mult).then_inc(mo_g, 1)

            for e in range(E):
                for i in range(4):
                    gate(4 * e + i)
                if e == 0:
                    dve.wait_ge(mo_wT, 1)
                    link(v.tensor_copy(wT[:], psum[:, 6, 0:TILES * E].rearrange("p (t e) -> p t e", e=E)))
                else:
                    dve.wait_ge(mo_acc, 2 * e)
                for c in range(2):
                    dve.wait_ge(mo_y, 2 * e + c + 1)
                    for i in range(4):
                        t = 4 * c + i
                        last = v.scalar_tensor_tensor(out=acc[:, t, :], in0=psum[:, 4 + c, i * P:(i + 1) * P],
                                                      scalar=wT[:, t, e:e + 1], in1=acc[:, t, :],
                                                      op0=ALU.mult, op1=ALU.add)
                    last.then_inc(mo_acc, 1)
            dve.wait_ge(mo_acc, 2 * E)
            norm(first + 2, lambda t: acc[:, t, :], TILES, 1e-5, 0.0, lambda t: yout[:, t, :], out_ready)


def kernel(**inputs):
    import numpy as np
    import concourse.bacc as bacc
    from concourse.bass_utils import run_bass_kernel_spmd as run

    def f(name):
        return np.ascontiguousarray(inputs[name])

    x, ctx = f("x"), f("ctx_1024")
    Wq, Wk, Wv, Wo = (f("L0_xattn_W" + c) for c in "qkvo")
    by_pair = lambda w: w.reshape(L, D, PAIRS, P).transpose(0, 2, 1, 3).reshape(L * PAIRS, D, P)
    WkT = Wk.reshape(L, D, PAIRS, P).transpose(0, 2, 3, 1).reshape(L * PAIRS, P, D)
    wqkv = np.stack([by_pair(Wq), WkT, by_pair(Wv)], axis=2)
    steps = [s // B % L for s in range(STEPS + 1)]
    W1, W3, W2 = f("L0_ffn_W1"), f("L0_ffn_W3"), f("L0_ffn_W2")
    W2T = W2.transpose(0, 2, 1).reshape(E, 2, P, D).transpose(0, 2, 1, 3).reshape(E, P, 2 * D)

    pos = np.arange(S, dtype=np.float32)
    freq = np.exp(-np.float32(np.log(10000.0)) * np.arange(0, SHD, 2, dtype=np.float32) / np.float32(SHD))
    angle = np.repeat(pos[:, None] * freq[None, :].astype(np.float32), 2, axis=1)
    sign = np.tile(np.array([-1.0, 1.0], np.float32), SHD // 2)
    wide = lambda a: np.tile(a.astype(np.float32), (1, 2 * SH)).reshape(FT, P, 2 * D).transpose(1, 0, 2)
    upper = np.where(np.arange(P)[None, :] > np.arange(P)[:, None], 1e30, 0.0).astype(np.float32)
    cmask = np.concatenate([upper, np.zeros((P, P), np.float32), upper], axis=1)
    hmask = np.where(np.arange(P)[:, None] // SHD == np.arange(SH)[None, :], -float(SHD) ** -0.5, 0.0)

    arrays = {
        "x": x, "xT": x.transpose(0, 2, 1), "fside": f("fside_BxSxS2_0"),
        "mask": f("mask_Bx1x1xS2_ff0").reshape(B, 1, T), "ctxT": ctx.transpose(0, 2, 1),
        "wqkvT": f("L0_attn_Wqkv").T, "woT": f("L0_attn_Wo").T,
        "wqkv": wqkv, "wo": Wo.reshape(L * PAIRS, P, D),
        "wth": f("L0_xattn_Wth").reshape(L, HID)[steps].reshape(1, -1),
        "bth": f("L0_xattn_bth")[steps].reshape(1, -1),
        "wto": f("L0_xattn_Wto").reshape(L, HID)[steps].reshape(1, -1),
        "bto": f("L0_xattn_bto").reshape(L)[steps].reshape(1, -1),
        "wf1": f("L0_xattn_Wf1"), "wf2": f("L0_xattn_Wf2").reshape(L, FB, P, D).transpose(0, 2, 1, 3),
        "bf1": f("L0_xattn_bf1").reshape(L, FB, P).transpose(0, 2, 1), "bf2": f("L0_xattn_bf2").reshape(L, 1, D),
        "wgT": f("L0_ffn_Wg").T,
        "wexp": np.concatenate([W1.transpose(0, 2, 1), W3.transpose(0, 2, 1), W2T], axis=2),
        "ident": np.eye(P, dtype=np.float32), "hmask": hmask.astype(np.float32), "cmask": cmask,
        "cos": wide(np.cos(angle)), "sin": wide(np.sin(angle) * sign),
    }
    arrays = {n: np.ascontiguousarray(a) for n, a in arrays.items()}
    nc = bacc.Bacc("TRN2", target_bir_lowering=False, num_devices=1)
    d = {n: nc.dram_tensor("in_" + n, a.shape, F32, kind="ExternalInput").ap() for n, a in arrays.items()}
    d["out"] = nc.dram_tensor("out", (B, S, D), F32, kind="ExternalOutput").ap()
    build(nc, d)
    return run(nc, [{"in_" + n: a for n, a in arrays.items()}], core_ids=[0]).results[0]["out"]
```

```python
from contextlib import ExitStack

import concourse.bass as bass
from concourse import mybir

F32 = mybir.dt.float32
F32R = mybir.dt.float32r
ALU = mybir.AluOpType
ACT = mybir.ActivationFunctionType

P = 128
B, S, D, T = 4, 256, 128, 1601
FT = S // P
L, HEADS, HD, HID = 4, 16, 64, 32
STEPS = L * B
PAIRS = HEADS // 2
UNITS = HEADS * FT
TT = -(-T // P)
LAST = T - (TT - 1) * P
TE = T + T % 2
TG = 4
CUT = 1024
FILT, FB = 512, 4
SH, SHD, GH = 16, 8, 4
SG = SH // GH
E, EH, CAP = 8, 256, 128
TOK = B * S
TILES = TOK // P
BIG = 3.0e38

START = ["XN1", "Q0", "QK0"]
FIRST = [(None, "VO0", "Q"), (None, "QK0", None), ("PV", None, None), ("PV", None, None)]
MIDDLE = [("PV", "VO", "Q"), ("PV", "QK", None), ("PV", "OT", None), ("PV", "Y", None)]
FINAL = [("PV", "VO", None), ("PV", "XN1", None), ("PV", "OT", "Q"), ("PV", "Y", "QK")]
TAIL = ["PV", "PV", "OT0", "Y0", "XN2", "H0", "H1", "Y2"]


def flat(kind):
    return [name for slot in kind for name in slot if name]


PER_PAIR = len(flat(MIDDLE))
BASE_MIDDLE = len(flat(FIRST)) - PER_PAIR
BASE_TAIL = BASE_MIDDLE + PER_PAIR * (PAIRS - 1) + len(flat(FINAL))
TASKS = BASE_TAIL + len(TAIL)
NORMS = 2
CHAIN_SA = 3 + 4
CHAIN_STEP = 2 * 4 + 1


QK_AT = flat(MIDDLE).index("QK")


def pairs_of(s, emit, each_j):
    def middle(p, half, kind, qk_task=None):
        emit(s, p, half, kind, BASE_MIDDLE + PER_PAIR * p, (BASE_MIDDLE + PER_PAIR * half) % 2,
             BASE_MIDDLE + PER_PAIR * (p - 1) + QK_AT if qk_task is None else qk_task)

    emit(s, 0, 0, FIRST, 0, 0, None)
    middle(1, 1, MIDDLE, flat(FIRST).index("QK0"))
    with each_j(1, PAIRS // 2 - 1) as j:
        for half in range(2):
            middle(2 * j + half, half, MIDDLE)
    middle(PAIRS - 2, 0, MIDDLE)
    middle(PAIRS - 1, 1, FINAL)


def pair_of(name, p, parity):
    if name in ("Q", "QK", "QK0"):
        return p + 1, 1 - parity
    if name in ("OT", "Y"):
        return p - 1, 1 - parity
    return p, parity


def weights_row(s, p):
    step, pair = (s, p) if p < PAIRS else (s + 1, p - PAIRS)
    return (step // B * PAIRS + pair) % (L * PAIRS)


def task_number(s, local):
    return len(START) + s * TASKS + local


def build(nc, d):
    with ExitStack() as ctx:
        def sb(name, shape):
            return ctx.enter_context(nc.sbuf_tensor(name, shape, F32))

        def sem(name):
            return ctx.enter_context(nc.semaphore(name))

        psum = ctx.enter_context(nc.psum_tensor("banks", [P, 8, 512], F32))

        ident = sb("ident", [P, P])
        half = sb("half", [P, 8])
        coef = sb("coef", [P, 2, (STEPS + 1) * HID])
        negc = sb("negc", [P, (STEPS + 1) * HID])
        nbto = sb("nbto", [P, STEPS + 1])
        xs = sb("xs", [P, B, FT, D])
        x_sa = sb("x_sa", [P, B, FT, D])
        dist = sb("dist", [P, 2, FT, T])
        maskb = sb("maskb", [P, T])
        relu = sb("relu", [P, 2, FT, T])
        nb_next = sb("nb_next", [P, FT, T])
        nb_cur = sb("nb_cur", [P, FT, T])
        ctxT = sb("ctxT", [P, 2, 2, TE])
        ctxT_in = sb("ctxT_in", [P, T])
        prob = sb("prob", [P, 2, T])
        probT = sb("probT", [P, 2, TT, P])
        ctxN = sb("ctxN", [P, TT, P])
        wpair = sb("wpair", [P, 2, 5, P])
        vo = sb("vo", [P, 2, 2, P])
        wf1 = sb("wf1", [P, FILT])
        wf2 = sb("wf2", [P, FB, D])
        bf1 = sb("bf1", [P, FB])
        bf2 = sb("bf2", [P, D])
        xcur = sb("xcur", [P, FT, D])
        xn = sb("xn", [P, FT, D])
        xnT = sb("xnT", [P, 2, S])
        q_sb = sb("q_sb", [P, 2, S])
        qk_sb = sb("qk_sb", [P, 2, 2, 2, S])
        nmA = sb("nmA", [P, 4])
        nm = sb("nm", [P, 4])
        rsum = sb("rsum", [P, 4])
        rinv = sb("rinv", [P, 4])
        On = sb("On", [P, 2, 4, P])
        OT = sb("OT", [P, 4, P])
        hT = sb("hT", [P, FB, S])
        bn = sb("bn", [P, TILES, 6])
        mv = sb("mv", [P, TILES, 2])
        vv = sb("vv", [P, TILES])
        sd = sb("sd", [P, TILES])
        rs = sb("rs", [P, TILES])

        def sems(*names):
            return [sem(n) for n in names]

        (const_ld, coef_ld, x_ld, xT_ld, out_st) = sems("const_ld", "coef_ld", "x_ld", "xT_ld", "out_st")
        (dist_ld, gate_ld, sa_ri, mo_n, carried) = sems("dist_ld", "gate_ld", "sa_ri", "mo_n", "carried")
        w_ld = sems("w_ld0", "w_ld1")
        (mask_ld, ctxT_ld, ctxN_ld, ffn_ld) = sems("mask_ld", "ctxT_ld", "ctxN_ld", "ffn_ld")
        (ctxT_high, ctxT_split, qk_high, x_kept) = sems("ctxT_high", "ctxT_split", "qk_high", "x_kept")
        exp_ld = sems("expert_ld0", "expert_ld1")
        (half_set, coef_neg, nmask_done, nb_copied, dve_chain, var_ready, std_ready, x_written,
         xn_done) = sems("half_set", "coef_neg", "nmask_done", "nb_copied", "dve_chain", "var_ready",
                         "std_ready", "x_written", "xn_done")
        (scores, scored, exped, turned, turn_copied, on_done, rinv_done, mm, mm_copied,
         relu_done, term_done) = sems("scores", "scored", "exped", "turned", "turn_copied",
                                      "on_done", "rinv_done", "mm", "mm_copied", "relu_done", "term_done")
        (sa_qkv, sa_rope, sa_turned, sa_qkT, sa_qm, sa_scores, sa_scored, sa_exp, sa_pT, sa_pTc,
         sa_pv, sa_on, sa_oT, sa_oTc, sa_y) = sems(
            "sa_qkv", "sa_rope", "sa_turned", "sa_qkT", "sa_qm", "sa_scores", "sa_scored", "sa_exp", "sa_pT",
            "sa_pTc", "sa_pv", "sa_on", "sa_oT", "sa_oTc", "sa_y")
        (mo_x, mo_xT, mo_xTc, mo_sc, mo_scc, mo_max, mo_e, mo_w, mo_wT, mo_wTc, mo_h, mo_sil, mo_g, mo_y,
         mo_acc, out_ready) = sems(
            "mo_x", "mo_xT", "mo_xTc", "mo_sc", "mo_scc", "mo_max", "mo_e", "mo_w", "mo_wT", "mo_wTc", "mo_h",
            "mo_sil", "mo_g", "mo_y", "mo_acc", "out_ready")

        sa_x = sb("sa_x", [P, FT, D])
        sa_xT = sb("sa_xT", [P, S])
        cos = sb("cos", [P, FT, 2 * D])
        sin = sb("sin", [P, FT, 2 * D])
        wqkvT = sb("wqkvT", [P, 3 * D])
        woT = sb("woT", [P, D])
        hmask = sb("hmask", [P, SH])
        cmask = sb("cmask", [P, 3 * P])
        flatT = probT[:, :, :, :].rearrange("p a b c -> p (a b c)")
        flatV = ctxN[:, :, :].rearrange("p a b -> p (a b)")
        qkr = flatT[:, 0:512].rearrange("p (a b) -> p a b", a=2)
        rot1 = flatT[:, 512:1024].rearrange("p (a b) -> p a b", a=2)
        rot2 = flatT[:, 1024:1536].rearrange("p (a b) -> p a b", a=2)
        v_sa = flatT[:, 1536:1792].rearrange("p (a b) -> p a b", a=2)
        qkT = flatT[:, 1792:2304].rearrange("p (a b) -> p a b", a=2)
        o_sa = flatT[:, 2304:2560].rearrange("p (a b) -> p a b", a=2)
        oT_sa = flatT[:, 2560:2816]
        qm = flatV[:, 0:1024].rearrange("p (a b) -> p a b", a=GH)
        flatP = prob[:, :, :].rearrange("p a b -> p (a b)")
        s_sa = flatP[:, 0:1536].rearrange("p (a b) -> p a b", a=GH)
        pT_sa = flatP[:, 1536:3072].rearrange("p (a b) -> p a b", a=GH)
        nm_sa = sb("nm_sa", [P, 2, GH])
        rs_sa = sb("rs_sa", [P, 2, GH])
        ri_sa = sb("ri_sa", [P, 2, GH])

        flatR = relu[:, :, :, :].rearrange("p a b c -> p (a b c)")
        flatD = dist[:, :, :, :].rearrange("p a b c -> p (a b c)")
        x2T = flatR[:, 0:1024]
        sil = flatR[:, 1024:3072].rearrange("p (a b) -> p a b", a=2)
        gat = flatR[:, 3072:5120].rearrange("p (a b) -> p a b", a=2)
        x2 = flatD[:, 0:1024].rearrange("p (a b) -> p a b", a=TILES)
        acc = flatD[:, 1024:2048].rearrange("p (a b) -> p a b", a=TILES)
        wexp = flatD[:, 2048:3584].rearrange("p (a b) -> p a b", a=2)
        wgT = flatD[:, 3584:3592]
        yout = flatD[:, 4096:5120].rearrange("p (a b) -> p a b", a=TILES)
        flatN = nb_next[:, :, :].rearrange("p a b -> p (a b)")
        flatC = nb_cur[:, :, :].rearrange("p a b -> p (a b)")
        sc8 = flatN[0:E, 0:1024]
        work = flatN[0:E, 1024:2048]
        ex8 = flatN[0:E, 2048:3072]
        keep = flatC[0:E, 0:1024]
        w8 = flatC[0:E, 1024:2048]
        top8 = sb("top8", [E, 8])
        sm8 = sb("sm8", [E, 4])
        tick = sb("tick", [P, 1])
        wT = sb("wT", [P, TILES, E])

        x_tiles = d["x"].rearrange("b (t p) d -> b p t d", p=P)
        f_tiles = d["fside"].rearrange("b (t p) k -> b p t k", p=P)

        def tiles_of(g):
            return range(4 * g, min(4 * g + 4, TT))

        def rows_of(t):
            return P if t < TT - 1 else LAST

        block = ctx.enter_context(nc.Block())

        def apart(eng):
            eng.sem_inc(carried, 1)

        @block.sync
        def _(sp):
            sp.sem_inc(scored, 2)
            sp.sem_inc(turned, 2 * TG)
            sp.sem_inc(turn_copied, 2)
            sp.sem_inc(on_done, 4)
            sp.sem_inc(mm_copied, 2)
            sp.sem_inc(term_done, 2)
            for dst, name in ((ident, "ident"), (wqkvT, "wqkvT"), (woT, "woT"), (hmask, "hmask"),
                              (cmask, "cmask"), (cos, "cos"), (sin, "sin")):
                sp.dma_start(dst[:], d[name]).then_inc(const_ld, 16)
            for dst, name in ((coef[:, 0], "wth"), (coef[:, 1], "bth"), (negc[:], "wto"), (nbto[:], "bto")):
                sp.dma_start(dst, d[name].to_broadcast(dst.shape)).then_inc(coef_ld, 16)
            sp.dma_start(maskb[:], d["mask"][0].to_broadcast([P, T])).then_inc(mask_ld, 16)
            sp.dma_start(dist[:, 0], f_tiles[0]).then_inc(dist_ld, 16)
            sp.wait_ge(nmask_done, 1)
            sp.dma_start(maskb[:], d["mask"][1].to_broadcast([P, T])).then_inc(mask_ld, 16)
            with sp.Fori(0, B) as b:
                sp.dma_start(sa_xT[:], d["xT"][b]).then_inc(xT_ld, 16)
                sp.dma_start(sa_x[:], x_tiles[b]).then_inc(x_ld, 16)
                sp.wait_ge(x_written, b + 1)
                apart(sp)
            sp.wait_ge(dist_ld, 16)
            sp.dma_start(dist[:, 1], f_tiles[1]).then_inc(dist_ld, 16)
            for p in range(2):
                sp.dma_start(wpair[:, p], d["wpair"][p]).then_inc(w_ld[p], 16)

            def load_ctxT(s):
                sp.dma_start(ctxT_in[:], d["ctxT"][s % B]).then_inc(ctxT_ld, 16)

            def load_ctxN(s):
                rows = d["ctx"][s % B]
                whole = (TT - 1) * P
                sp.dma_start(ctxN[:, 0:TT - 1], rows[0:whole].rearrange("(t p) d -> p t d", p=P)).then_inc(ctxN_ld, 16)
                sp.dma_start(ctxN[0:LAST, TT - 1], rows[whole:T]).then_inc(ctxN_ld, 16)

            def load_ffn(s):
                layer = s // B % L
                for dst, name in ((wf1, "wf1"), (wf2, "wf2"), (bf1, "bf1")):
                    sp.dma_start(dst[:], d[name][layer]).then_inc(ffn_ld, 16)
                sp.dma_start(bf2[:], d["bf2"][layer].to_broadcast([P, D])).then_inc(ffn_ld, 16)

            load_ctxT(0)
            load_ctxN(0)
            load_ffn(0)
            with sp.Fori(0, STEPS) as s:
                sp.wait_ge(ctxT_split, s + 1)
                apart(sp)
                load_ctxT(s + 1)
                sp.wait_ge(dist_ld, 16 * (s + 2))
                apart(sp)
                sp.wait_ge(relu_done, HID * (s + 1))
                sp.dma_start(dist[:, s % 2], f_tiles[(s + 2) % B]).then_inc(dist_ld, 16)
                sp.wait_ge(term_done, HID * (s + 1) + 3)
                sp.dma_start(maskb[:], d["mask"][(s + 2) % B].to_broadcast([P, T])).then_inc(mask_ld, 16)
                for p in range(PAIRS):
                    at = (flat(FIRST).index("VO0") if p == 0 else
                          BASE_MIDDLE + PER_PAIR * p + flat(MIDDLE).index("VO"))
                    sp.wait_ge(mm, task_number(s, at) + 1)
                    sp.dma_start(wpair[:, p % 2], d["wpair"][weights_row(s, p + 2)]).then_inc(w_ld[p % 2], 16)
                sp.wait_ge(mm, task_number(s, BASE_TAIL + 1) + 1)
                load_ctxN(s + 1)
                sp.wait_ge(x_written, B + s + 1)
                load_ffn(s + 1)

            sp.wait_ge(mo_x, 1)
            sp.dma_start(wgT, d["wgT"]).then_inc(gate_ld, 16)
            for e in range(2):
                sp.dma_start(wexp[:, e], d["wexp"][e]).then_inc(exp_ld[e], 16)
            for e in range(2, E):
                sp.wait_ge(mo_y, 2 * (e - 1))
                sp.dma_start(wexp[:, e % 2], d["wexp"][e]).then_inc(exp_ld[e % 2], 16)
            sp.wait_ge(out_ready, 1)
            sp.dma_start(d["out"].rearrange("b (t p) d -> p (b t) d", p=P), yout).then_inc(out_st, 16)
            sp.wait_ge(out_st, 16)
            sp.wait_ge(ctxT_ld, 16 * (STEPS + 1))
            sp.wait_ge(ctxN_ld, 16 * 2 * (STEPS + 1))
            sp.wait_ge(ffn_ld, 16 * 4 * (STEPS + 1))
            for ld in w_ld:
                sp.wait_ge(ld, 16 * (STEPS * PAIRS // 2 + 1))

        @block.gpsimd
        def _(pool):
            nc.gpsimd.memset(ctxT[:, :, :, T:TE], 0.0)
            nc.gpsimd.memset(half[:], 0.5).then_inc(half_set, 1)
            pool.wait_ge(half_set, 1)

            def root(n, width):
                pool.wait_ge(var_ready, n + 1)
                nc.gpsimd.tensor_tensor(sd[:, 0:width], vv[:, 0:width], half[:, 0:width], ALU.pow
                                        ).then_inc(std_ready, 1)

            def split_ctxT(s, parity):
                high, low = ctxT[:, parity, 0, 0:T], ctxT[:, parity, 1, 0:T]
                pool.wait_ge(ctxT_ld, 16 * (s + 1))
                nc.gpsimd.tensor_copy(high.bitcast(F32R), ctxT_in[:]).then_inc(ctxT_high, 1)
                pool.wait_ge(ctxT_high, s + 1)
                nc.gpsimd.tensor_tensor(low.bitcast(F32R), ctxT_in[:], high, ALU.subtract).then_inc(ctxT_split, 1)

            with pool.Fori(0, B) as n:
                root(n, FT)
            root(B, FT)
            split_ctxT(0, 0)
            with pool.Fori(0, STEPS) as s:
                pool.wait_ge(scores, 2 * UNITS * s + 2)
                split_ctxT(s + 1, (s + 1) % 2)
                for i in range(NORMS):
                    root(B + 1 + NORMS * s + i, FT)
            for n in range(3):
                root(B + 1 + NORMS * STEPS + n, TILES)

        @block.tensor
        def _(pe):
            mat = nc.tensor.matmul

            def turn(out, in_, k=P):
                return nc.tensor.transpose(out, in_, ident[0:k, 0:k])

            pe.wait_ge(const_ld, 16 * 7)
            with pe.Fori(0, B) as b:
                pe.wait_ge(xT_ld, 16 * (b + 1))
                for ft in range(FT):
                    mat(psum[:, 6 + ft, 0:3 * D], sa_xT[:, ft * P:(ft + 1) * P], wqkvT[:], start=True, stop=True
                        ).then_inc(sa_qkv, 1)
                pe.wait_ge(sa_rope, b + 1)
                for a in range(2):
                    for ft in range(FT):
                        last = turn(psum[:, 6, (2 * a + ft) * P:(2 * a + ft + 1) * P], qkr[:, ft, a * D:(a + 1) * D])
                last.then_inc(sa_turned, 1)
                with pe.Fori(0, SG) as g:
                    group = b * SG + g
                    for h in range(GH):
                        pe.wait_ge(sa_qm, GH * group + h + 1)
                        mat(psum[:, h, 0:P], qm[:, h, 0:P], qkT[:, 1, 0:P], start=True, stop=True)
                        mat(psum[:, h, P:3 * P], qm[:, h, P:2 * P], qkT[:, 1, :], start=True, stop=True
                            ).then_inc(sa_scores, 1)
                    for h in range(GH):
                        pe.wait_ge(sa_exp, GH * group + h + 1)
                        if h >= 2:
                            pe.wait_ge(sa_pTc, GH * group + h - 1)
                        for c in range(3):
                            last = turn(psum[:, 4 + h % 2, c * P:(c + 1) * P], s_sa[:, h, c * P:(c + 1) * P])
                        last.then_inc(sa_pT, 1)
                    pe.wait_ge(sa_pTc, GH * group + GH)
                    for h in range(GH):
                        vs = [v_sa[:, ft, bass.ds(g * (GH * SHD) + h * SHD, SHD)] for ft in range(FT)]
                        o = [psum[:, 7, (a * GH + h) * SHD:(a * GH + h + 1) * SHD] for a in range(2)]
                        mat(o[0], pT_sa[:, h, 0:P], vs[0], start=True, stop=True)
                        mat(o[1], pT_sa[:, h, P:2 * P], vs[0], start=True, stop=False)
                        last = mat(o[1], pT_sa[:, h, 2 * P:3 * P], vs[1], start=False, stop=True)
                    last.then_inc(sa_pv, 1)
                pe.wait_ge(sa_on, (b + 1) * SG)
                for ft in range(FT):
                    last = turn(psum[:, 6, ft * P:(ft + 1) * P], o_sa[:, ft, :])
                last.then_inc(sa_oT, 1)
                pe.wait_ge(sa_oTc, b + 1)
                for ft in range(FT):
                    last = mat(psum[:, 7, ft * P:(ft + 1) * P], oT_sa[:, ft * P:(ft + 1) * P], woT[:],
                               start=True, stop=True)
                last.then_inc(sa_y, 1)

            def task(kind, s, local, bank, p, parity):
                n, ps = task_number(s, local), psum[:, bank, :]
                pe.wait_ge(mm_copied, n + (2 if kind[-1] == "0" or kind in ("XN2", "Y2") else 1))
                if kind[0] == "X":
                    pe.wait_ge(xn_done, 1 if isinstance(s, int) else NORMS * (s + 1) + (1 if kind == "XN2" else 0))
                    for ft in range(FT):
                        last = turn(ps[:, ft * P:(ft + 1) * P], xn[:, ft, :])
                elif kind in ("Q", "Q0"):
                    pe.wait_ge(w_ld[parity], 16 * (s * (PAIRS // 2) + p // 2 + 1))
                    last = mat(ps[:, 0:S], wpair[:, parity, 0, :], xnT[:, 0], start=True, stop=True)
                elif kind in ("QK", "QK0"):
                    last = mat(ps, wpair[:, parity, 1, :], q_sb[:, :, :].rearrange("p h c -> p (h c)"),
                               start=True, stop=True)
                elif kind in ("VO", "VO0"):
                    last = mat(ps[:, 0:2 * P], wpair[:, parity, 2, :],
                               wpair[:, parity, 3:5, :].rearrange("p h c -> p (h c)"), start=True, stop=True)
                elif kind in ("OT", "OT0"):
                    pe.wait_ge(on_done, 4 + s * UNITS + 4 * (p + 1))
                    for k in range(4):
                        last = turn(ps[:, k * P:(k + 1) * P], On[:, parity, k, :])
                elif kind in ("Y", "Y0"):
                    for ft in range(FT):
                        for h in range(2):
                            last = mat(ps[:, ft * P:(ft + 1) * P], OT[:, 2 * h + ft, :], vo[:, parity, h, :],
                                       start=(h == 0), stop=(h == 1))
                elif kind[0] == "H":
                    if kind == "H0":
                        pe.wait_ge(ffn_ld, 16 * 4 * (s + 1))
                    for i in range(2):
                        f = 2 * int(kind[1]) + i
                        last = mat(ps[:, i * S:(i + 1) * S], wf1[:, f * P:(f + 1) * P], xnT[:, 1],
                                   start=True, stop=True)
                else:
                    for ft in range(FT):
                        for f in range(FB):
                            last = mat(ps[:, ft * P:(ft + 1) * P], hT[:, f, ft * P:(ft + 1) * P], wf2[:, f, :],
                                       start=(f == 0), stop=(f == FB - 1))
                last.then_inc(mm, 1)

            def unit_scores(s, u, k, parity, qk_task, of_step):
                n = s * UNITS + u
                if qk_task is not None:
                    pe.wait_ge(mm_copied, task_number(s, qk_task) + 3)
                for c, (lo, hi) in enumerate(((0, CUT), (CUT, TE))):
                    pe.wait_ge(scored, 2 * n + c + 1)
                    for i, a in enumerate(range(lo, hi, 512)):
                        z = min(a + 512, hi)
                        for part, (qp, cp) in enumerate(((1, 0), (0, 1), (0, 0))):
                            last = mat(psum[:, 2 * c + i, 0:z - a],
                                       qk_sb[:, parity, qp, k // 2, (k % 2) * P:(k % 2 + 1) * P].bitcast(F32R),
                                       ctxT[:, of_step, cp, a:z].bitcast(F32R),
                                       start=(part == 0), stop=(part == 2))
                    last.then_inc(scores, 1)

            def unit_turn(s, u, k, groups):
                n = s * UNITS + u
                for g in groups:
                    if g == 0:
                        pe.wait_ge(exped, n + 1)
                    pe.wait_ge(turn_copied, TG * n + g + 1)
                    for i, t in enumerate(tiles_of(g)):
                        m = rows_of(t)
                        last = turn(psum[0:m, 4 + g % 2, i * P:(i + 1) * P], prob[:, k % 2, t * P:t * P + m])
                    last.then_inc(turned, 1)

            def unit_pv(s, u, k, local, bank):
                n = s * UNITS + u
                pe.wait_ge(turn_copied, TG * (n + 1) + 2)
                pe.wait_ge(mm_copied, task_number(s, local) + 1)
                for t in range(TT):
                    m = rows_of(t)
                    last = mat(psum[:, bank, 0:P], probT[0:m, k % 2, t, :], ctxN[0:m, t, :],
                               start=(t == 0), stop=(t == TT - 1))
                last.then_inc(mm, 1)

            def pair(s, p, parity, kind, base, odd, qk_task):
                off = 0
                for k in range(4):
                    u = 4 * p + k
                    if kind is not FIRST or k >= 1:
                        unit_scores(s, u, k, parity, qk_task if k == 0 else None, s % 2)
                        unit_turn(s, u - 1, (k - 1) % 4, (0, 1))
                    if kind[k][0]:
                        if kind is FIRST and k == 2:
                            pe.wait_ge(ctxN_ld, 32 * (s + 1))
                        unit_pv(s, u - 2, (k - 2) % 4, base + off, 6 + (odd + off) % 2)
                        off += 1
                    if kind is not FIRST or k >= 1:
                        unit_turn(s, u - 1, (k - 1) % 4, (2, 3))
                    for name in kind[k][1:]:
                        if name:
                            task(name, s, base + off, 6 + (odd + off) % 2, *pair_of(name, p, parity))
                            off += 1

            def first_scores(s):
                pe.wait_ge(ctxT_split, s + 1)
                unit_scores(s, 0, 0, 0, None, s % 2)

            for i, name in enumerate(START):
                task(name, -1, TASKS - len(START) + i, 6 + i % 2, PAIRS, 0)
            pe.wait_ge(mm_copied, len(START) + 2)
            first_scores(0)
            with pe.Fori(0, STEPS) as s:
                pairs_of(s, pair, pe.Fori)
                for i, name in enumerate(TAIL):
                    at = (BASE_TAIL + i, 6 + (BASE_TAIL + i) % 2)
                    if name == "PV":
                        unit_pv(s, UNITS - 2 + i, 2 + i, *at)
                        if i == 0:
                            unit_turn(s, UNITS - 1, 3, range(TG))
                    else:
                        task(name, s, *at, PAIRS - 1, 1)
                    if name == "Y0":
                        first_scores(s + 1)

            pe.wait_ge(mo_x, 1)
            for t in range(TILES):
                last = turn(psum[:, t // 4, t % 4 * P:(t % 4 + 1) * P], x2[:, t, :])
            last.then_inc(mo_xT, 1)
            pe.wait_ge(mo_xTc, 1)
            pe.wait_ge(gate_ld, 16)
            for c in range(2):
                last = mat(psum[0:E, 2 + c, :], wgT, x2T[:, c * 512:(c + 1) * 512], start=True, stop=True)
            last.then_inc(mo_sc, 1)
            for e in range(E):
                if e == 0:
                    pe.wait_ge(mo_scc, 1)
                pe.wait_ge(exp_ld[e % 2], 16 * (e // 2 + 1))
                for hh in range(2):
                    for c in range(2):
                        i = 4 * e + 2 * hh + c
                        if i >= 2:
                            pe.wait_ge(mo_g, i - 1)
                        for a in range(2):
                            last = mat(psum[:, 2 * (i % 2) + a, :],
                                       wexp[:, e % 2, a * EH + hh * P:a * EH + (hh + 1) * P],
                                       x2T[:, c * 512:(c + 1) * 512], start=True, stop=True)
                        last.then_inc(mo_h, 1)
                if e == 0:
                    pe.wait_ge(mo_w, 1)
                    for t in range(TILES):
                        last = turn(psum[:, 6, t * E:(t + 1) * E], w8[:, t * P:(t + 1) * P], E)
                    last.then_inc(mo_wT, 1)
                pe.wait_ge(mo_g, 4 * (e + 1))
                for c in range(2):
                    if e >= 1:
                        pe.wait_ge(mo_acc, 2 * (e - 1) + c + 1)
                    for i in range(4):
                        t = 4 * c + i
                        for hh in range(2):
                            last = mat(psum[:, 4 + c, i * P:(i + 1) * P], gat[:, hh, t * P:(t + 1) * P],
                                       wexp[:, e % 2, 2 * EH + hh * P:2 * EH + (hh + 1) * P],
                                       start=(hh == 0), stop=(hh == 1))
                    last.then_inc(mo_y, 1)

        @block.scalar
        def _(act):
            fun = nc.scalar.activation

            def bias_relu(n, buf, slot, first):
                act.wait_ge(term_done, n + 1)
                fun(relu[:, buf], slot, ACT.Relu, bias=coef[:, 1, bass.ds(n, 1)],
                    scale=coef[:, 0, bass.ds(n, 1)]).then_inc(relu_done, 1)

            act.wait_ge(coef_ld, 16 * 4)
            act.wait_ge(dist_ld, 16)
            with act.Fori(0, B * SG) as group:
                for h in range(GH):
                    for a in range(2):
                        act.wait_ge(sa_scored, 2 * GH * group + 2 * h + a + 1)
                        part = s_sa[:, h, 0:P] if a == 0 else s_sa[:, h, P:3 * P]
                        last = fun(part, part, ACT.Exp, scale=-1.0, bias=nm_sa[:, a, h:h + 1],
                                   accum_out=rs_sa[:, a, h:h + 1])
                    last.then_inc(sa_exp, 1)
                for i in range(2):
                    bias_relu(2 * group + i, i, dist[:, 0], False)
                for h in range(GH):
                    act.wait_ge(sa_pT, GH * group + h + 1)
                    fun(pT_sa[:, h, :], psum[:, 4 + h % 2, 0:3 * P], ACT.Copy).then_inc(sa_pTc, 1)

            def unit_exp(s, u, k):
                n = s * UNITS + u
                act.wait_ge(scored, 2 * n + 4)
                fun(prob[:, k % 2, :], prob[:, k % 2, :], ACT.Exp, scale=-1.0, bias=nm[:, k:k + 1],
                    accum_out=rsum[:, k:k + 1]).then_inc(exped, 1)

            def unit_copy(s, u, k, groups):
                n = s * UNITS + u
                for g in groups:
                    act.wait_ge(turned, TG * (n + 2) + g + 1)
                    if g == 0:
                        act.wait_ge(on_done, n + 3)
                    ts = tiles_of(g)
                    m = rows_of(ts[-1])
                    fun(probT[0:m, k % 2, ts[0]:ts[-1] + 1, :],
                        psum[0:m, 4 + g % 2, 0:len(ts) * P].rearrange("p (t q) -> p t q", q=P), ACT.Copy
                        ).then_inc(turn_copied, 1)

            def pair(s, p, parity, kind, base, odd, qk_task):
                for k in range(4):
                    u = 4 * p + k
                    go = kind is not FIRST or k >= 1
                    bias_relu((s + 1) * HID + u, k % 2, dist[:, (s + 1) % 2], False)
                    if go:
                        unit_copy(s, u - 1, (k - 1) % 4, (0, 1))
                    unit_exp(s, u, k)
                    if go:
                        unit_copy(s, u - 1, (k - 1) % 4, (2, 3))

            with act.Fori(0, STEPS) as s:
                act.wait_ge(dist_ld, 16 * (s + 2))
                pairs_of(s, pair, act.Fori)
                unit_copy(s, UNITS - 1, 3, range(TG))

            act.wait_ge(mo_max, 1)
            fun(ex8, sc8, ACT.Exp, bias=sm8[:, 0:1]).then_inc(mo_e, 1)
            for i in range(4 * E):
                act.wait_ge(mo_h, i + 1)
                if i >= 2:
                    act.wait_ge(mo_g, i - 1)
                fun(sil[:, i % 2, 0:512], psum[:, 2 * (i % 2), :], ACT.Silu).then_inc(mo_sil, 1)

        @block.vector
        def _(dve):
            v = nc.vector
            chain = {"base": 0, "n": 0}

            def link(ins):
                chain["n"] += 1
                ins.then_inc(dve_chain, 1)
                dve.wait_ge(dve_chain, chain["base"] + chain["n"])

            def norm(n, src, width, before, after, out, done):
                for t in range(width):
                    last = v.bn_stats(bn[:, t, :], src(t))
                link(last)
                apart(dve)
                for t in range(width):
                    last = v.bn_aggr(mv[:, t, :], bn[:, t, :])
                link(last)
                v.tensor_scalar(vv[:, 0:width], mv[:, 0:width, 1], before, None, ALU.add).then_inc(var_ready, 1)
                dve.wait_ge(std_ready, n + 1)
                link(v.tensor_scalar(rs[:, 0:width], sd[:, 0:width], after, None, ALU.add))
                link(v.reciprocal(rs[:, 0:width], rs[:, 0:width]))
                for t in range(width):
                    last = v.tensor_scalar(out(t), src(t), mv[:, t, 0:1], rs[:, t:t + 1], ALU.subtract, ALU.mult)
                last.then_inc(done, 1)

            def bias_term(n, buf, first, tiles=range(FT), out=nb_next):
                if 0 in tiles:
                    dve.wait_ge(relu_done, n + 1)
                    dve.wait_ge(term_done, n + 2)
                for ft in tiles:
                    start = maskb[:, :] if first else nb_next[:, ft, :]
                    last = v.scalar_tensor_tensor(out=out[:, ft, :], in0=relu[:, buf, ft, :],
                                                  scalar=negc[:, bass.ds(n, 1)], in1=start,
                                                  op0=ALU.mult, op1=ALU.add)
                if FT - 1 in tiles:
                    last.then_inc(term_done, 1)

            v.memset(q_sb[:], 0.0)
            dve.wait_ge(coef_ld, 16 * 4)
            v.tensor_scalar(negc[:], negc[:], -1.0, None, ALU.mult)
            link(v.tensor_scalar(nbto[:], nbto[:], -1.0, None, ALU.mult))
            dve.wait_ge(mask_ld, 16)
            for ft in range(FT):
                last = v.tensor_scalar(nb_next[:, ft, :], maskb[:], -1.0, nbto[:, 0:1], ALU.mult, ALU.add)
            last.then_inc(nmask_done, 1)
            dve.wait_ge(nmask_done, 1)
            dve.wait_ge(const_ld, 16 * 7)
            setup = chain["n"]

            with dve.Fori(0, B) as b:
                chain["base"], chain["n"] = setup + b * CHAIN_SA, 0
                dve.wait_ge(sa_qkv, FT * (b + 1))
                for ft in range(FT):
                    ps = psum[:, 6 + ft, 0:2 * D]
                    v.tensor_tensor(rot1[:, ft, :], ps, cos[:, ft, :], ALU.mult)
                    two = [x.rearrange("p (i two) -> p i two", two=2) for x in (rot2[:, ft, :], ps, sin[:, ft, :])]
                    for a in range(2):
                        last = v.tensor_tensor(two[0][:, :, a], two[1][:, :, 1 - a], two[2][:, :, a], ALU.mult)
                    v.tensor_copy(v_sa[:, ft, :], psum[:, 6 + ft, 2 * D:3 * D])
                link(last)
                v.tensor_tensor(qkr, rot1, rot2, ALU.add).then_inc(sa_rope, 1)
                dve.wait_ge(sa_turned, b + 1)
                link(v.tensor_copy(qkT, psum[:, 6, :].rearrange("p (a c) -> p a c", a=2)))
                apart(dve)
                with dve.Fori(0, SG) as g:
                    group = b * SG + g
                    for h in range(GH):
                        v.tensor_scalar(qm[:, h, :], qkT[:, 0, :], hmask[:, bass.ds(g * GH + h, 1)], None, ALU.mult
                                        ).then_inc(sa_qm, 1)
                    for h in range(GH):
                        dve.wait_ge(sa_scores, GH * group + h + 1)
                        for a, (lo, hi) in enumerate(((0, P), (P, 3 * P))):
                            apart(dve)
                            v.tensor_tensor_reduce(out=s_sa[:, h, lo:hi], in0=psum[:, h, lo:hi],
                                                   in1=cmask[:, lo:hi], scale=1.0, scalar=BIG, op0=ALU.add,
                                                   op1=ALU.min, accum_out=nm_sa[:, a, h:h + 1]).then_inc(sa_scored, 1)
                    for i in range(2):
                        bias_term(2 * group + i, i, False)
                    dve.wait_ge(sa_pv, group + 1)
                    v.reciprocal(ri_sa[:], rs_sa[:]).then_inc(sa_ri, 1)
                    dve.wait_ge(sa_ri, group + 1)
                    v.tensor_tensor(o_sa[:, :, bass.ds(g * GH * SHD, GH * SHD)].rearrange("p a (h c) -> p a h c", c=SHD),
                                    psum[:, 7, 0:2 * GH * SHD].rearrange("p (a h c) -> p a h c", a=2, c=SHD),
                                    ri_sa[:].rearrange("p a (h o) -> p a h o", o=1).to_broadcast([P, 2, GH, SHD]),
                                    ALU.mult).then_inc(sa_on, 1)
                dve.wait_ge(sa_oT, b + 1)
                v.tensor_copy(oT_sa, psum[:, 6, 0:S]).then_inc(sa_oTc, 1)
                dve.wait_ge(sa_y, b + 1)
                dve.wait_ge(x_ld, 16 * (b + 1))
                link(v.tensor_tensor(xcur[:], sa_x[:], psum[:, 7, 0:S].rearrange("p (a c) -> p a c", a=2), ALU.add))
                norm(b, lambda t: xcur[:, t, :], FT, 1e-5, 0.0, lambda t: xs[:, b, t, :], x_written)
                chain_sa = chain["n"]
            assert chain_sa == CHAIN_SA, chain_sa
            after_sa = setup + B * CHAIN_SA

            def copy(kind, s, local, bank, p, parity):
                n, ps = task_number(s, local), psum[:, bank, :]
                dve.wait_ge(mm, n + 1)
                if kind[0] == "X":
                    last = v.tensor_copy(xnT[:, int(kind == "XN2")], ps[:, 0:S])
                elif kind in ("Q", "Q0"):
                    for h in range(2):
                        k = slice(h * HD, (h + 1) * HD)
                        last = v.tensor_scalar(q_sb[k, h, :], ps[k, 0:S], -float(HD) ** -0.5, None, ALU.mult)
                elif kind in ("QK", "QK0"):
                    high, low = (qk_sb[:, parity, i].rearrange("p h c -> p (h c)") for i in range(2))
                    v.tensor_copy(high.bitcast(F32R), ps).then_inc(qk_high, 1)
                    dve.wait_ge(qk_high, 1 if isinstance(s, int) else s * PAIRS + p + 1)
                    last = v.tensor_tensor(low.bitcast(F32R), ps, high, ALU.subtract)
                elif kind in ("VO", "VO0"):
                    last = v.tensor_copy(vo[:, parity], ps[:, 0:2 * P].rearrange("p (h c) -> p h c", h=2))
                elif kind in ("OT", "OT0"):
                    last = v.tensor_copy(OT[:], ps.rearrange("p (k c) -> p k c", k=4))
                elif kind in ("Y", "Y0"):
                    before = xs[:, s % B] if isinstance(p, int) and p == 0 else xcur[:]
                    last = v.tensor_tensor(xcur[:], before, ps[:, 0:S].rearrange("p (a c) -> p a c", a=2), ALU.add)
                elif kind[0] == "H":
                    for i in range(2):
                        f = 2 * int(kind[1]) + i
                        last = v.tensor_scalar(hT[:, f, :], ps[:, i * S:(i + 1) * S], bf1[:, f:f + 1], 0.0,
                                               ALU.add, ALU.max)
                last.then_inc(mm_copied, 1)

            def unit_add(s, u, k):
                n = s * UNITS + u
                dve.wait_ge(turned, TG * (n + 1))
                for c, (lo, hi) in enumerate(((0, CUT), (CUT, T))):
                    dve.wait_ge(scores, 2 * n + c + 1)
                    if c == 1:
                        dve.wait_ge(scored, 2 * n + 3)
                    apart(dve)
                    v.tensor_tensor_reduce(
                        out=prob[:, k % 2, lo:hi],
                        in0=psum[:, 2 * c:2 * c + 2, :].rearrange("p a b -> p (a b)")[:, 0:hi - lo],
                        in1=nb_cur[:, k % 2, lo:hi], scale=1.0, scalar=BIG if c == 0 else nmA[:, k:k + 1],
                        op0=ALU.add, op1=ALU.min, accum_out=(nmA if c == 0 else nm)[:, k:k + 1]).then_inc(scored, 1)

            def unit_norm(s, u, k, local, bank, parity):
                n = s * UNITS + u
                dve.wait_ge(mm, task_number(s, local) + 1)
                v.reciprocal(rinv[:, k:k + 1], rsum[:, k:k + 1]).then_inc(rinv_done, 1)
                dve.wait_ge(rinv_done, n + 1)
                v.tensor_scalar(On[:, parity, k, :], psum[:, bank, 0:P], rinv[:, k:k + 1], None, ALU.mult
                                ).then_inc(mm_copied, 1)
                v.memset(tick[:], 0.0).then_inc(on_done, 1)

            def pair(s, p, parity, kind, base, odd, qk_task):
                off = 0
                for k in range(4):
                    u = 4 * p + k
                    unit_add(s, u, k)
                    term = ((s + 1) * HID + u, k % 2, kind is FIRST and k == 0)
                    out = nb_cur if kind is FINAL and k == 3 else nb_next
                    bias_term(*term, [0], out)
                    if kind is FINAL and k == 0:
                        dve.wait_ge(x_written, s + 2)
                        norm(B + 1 + NORMS * s, lambda t: xs[:, (s + 1) % B, t, :], FT, 0.0, 1e-6,
                             lambda t: xn[:, t, :], xn_done)
                    for name in kind[k]:
                        if name == "PV":
                            unit_norm(s, u - 2, (k - 2) % 4, base + off, 6 + (odd + off) % 2,
                                      parity if k >= 2 else 1 - parity)
                        elif name:
                            copy(name, s, base + off, 6 + (odd + off) % 2, *pair_of(name, p, parity))
                        off += 1 if name else 0
                    bias_term(*term, [1], out)

            chain["base"], chain["n"] = after_sa, 0
            dve.wait_ge(x_written, B)
            v.tensor_copy(x_sa[:], xs[:]).then_inc(x_kept, 1)
            norm(B, lambda t: xs[:, 0, t, :], FT, 0.0, 1e-6, lambda t: xn[:, t, :], xn_done)
            dve.wait_ge(term_done, HID + 2)
            v.tensor_copy(nb_cur[:], nb_next[:]).then_inc(nb_copied, 1)
            for i, name in enumerate(START):
                copy(name, -1, TASKS - len(START) + i, 6 + i % 2, PAIRS, 0)
            after_start = after_sa + chain["n"]
            with dve.Fori(0, STEPS) as s:
                chain["base"], chain["n"] = after_start + s * CHAIN_STEP, 0
                dve.wait_ge(nb_copied, 1)
                dve.wait_ge(term_done, HID * (s + 1) + 2)
                dve.wait_ge(mask_ld, 16 * (s + 2))
                v.tensor_scalar(maskb[:], maskb[:], -1.0, nbto[:, bass.ds(s + 1, 1)], ALU.mult, ALU.add
                                ).then_inc(nmask_done, 1)
                dve.wait_ge(nmask_done, s + 2)
                pairs_of(s, pair, dve.Fori)
                for i, name in enumerate(TAIL):
                    local, bank = BASE_TAIL + i, 6 + (BASE_TAIL + i) % 2
                    n = task_number(s, local)
                    if name == "XN2":
                        dve.wait_ge(mm_copied, n + 2)
                        norm(B + 2 + NORMS * s, lambda t: xcur[:, t, :], FT, 0.0, 1e-6, lambda t: xn[:, t, :],
                             xn_done)
                        dve.wait_ge(xn_done, 1 + NORMS * (s + 1))
                        dve.wait_ge(ffn_ld, 16 * 4 * (s + 1))
                        link(v.tensor_tensor(xcur[:], xcur[:],
                                             bf2[:].rearrange("p (o c) -> p o c", o=1).to_broadcast([P, FT, D]),
                                             ALU.add))
                    if name == "Y2":
                        dve.wait_ge(mm, n + 1)
                        v.tensor_tensor(xs[:, s % B], xcur[:],
                                        psum[:, bank, 0:S].rearrange("p (a c) -> p a c", a=2), ALU.add
                                        ).then_inc(mm_copied, 1)
                        v.memset(tick[:], 0.0).then_inc(x_written, 1)
                    elif name == "PV":
                        unit_norm(s, UNITS - 2 + i, 2 + i, local, bank, 1)
                    else:
                        copy(name, s, local, bank, PAIRS - 1, 1)
                chain_step = chain["n"]
            assert chain_step == CHAIN_STEP, chain_step
            chain["base"], chain["n"] = after_start + STEPS * CHAIN_STEP, 0

            first = B + 1 + NORMS * STEPS
            dve.wait_ge(x_written, B + STEPS)
            dve.wait_ge(dist_ld, 16 * (STEPS + 2))
            dve.wait_ge(relu_done, HID * (STEPS + 1))
            dve.wait_ge(x_kept, 1)
            norm(first, lambda t: xs[:, t // FT, t % FT, :], TILES, 0.0, 1e-6, lambda t: x2[:, t, :], mo_n)
            dve.wait_ge(mo_n, 1)
            link(v.tensor_tensor(acc.rearrange("p t d -> p (t d)"), x2.rearrange("p t d -> p (t d)"),
                                 x_sa[:].rearrange("p b t d -> p (b t d)"), ALU.add))
            norm(first + 1, lambda t: acc[:, t, :], TILES, 1e-5, 0.0, lambda t: x2[:, t, :], mo_x)
            dve.wait_ge(mo_x, 1)
            link(v.tensor_copy(acc, x2))

            dve.wait_ge(mo_xT, 1)
            v.tensor_copy(x2T, psum[:, 0:2, :].rearrange("p a b -> p (a b)")).then_inc(mo_xTc, 1)
            dve.wait_ge(mo_sc, 1)
            v.tensor_copy(sc8, psum[0:E, 2:4, :].rearrange("p a b -> p (a b)"))
            link(v.tensor_copy(work, psum[0:E, 2:4, :].rearrange("p a b -> p (a b)")))
            for r in range(CAP // 8):
                link(v.max(top8[:], work))
                if r == 0:
                    v.tensor_scalar(sm8[:, 0:1], top8[:, 0:1], -1.0, None, ALU.mult).then_inc(mo_max, 1)
                    v.memset(tick[:], 0.0).then_inc(mo_scc, 1)
                link(v.match_replace(out=work, in_to_replace=top8[:], in_values=work, imm_value=-BIG))
            link(v.tensor_tensor(keep, work, sc8, ALU.not_equal))
            dve.wait_ge(mo_e, 1)
            link(v.tensor_tensor_reduce(out=w8, in0=ex8, in1=keep, scale=1.0, scalar=0.0, op0=ALU.mult,
                                        op1=ALU.add, accum_out=sm8[:, 1:2]))
            link(v.reciprocal(sm8[:, 2:3], sm8[:, 1:2]))
            v.tensor_scalar(w8, w8, sm8[:, 2:3], None, ALU.mult).then_inc(mo_w, 1)

            def gate(i):
                hh, c = i // 2 % 2, i % 2
                dve.wait_ge(mo_sil, i + 1)
                if i >= 4 and i % 4 == 0:
                    dve.wait_ge(mo_y, 2 * (i // 4))
                v.tensor_tensor(gat[:, hh, c * 512:(c + 1) * 512], sil[:, i % 2, 0:512],
                                psum[:, 2 * (i % 2) + 1, :], ALU.mult).then_inc(mo_g, 1)

            for e in range(E):
                for i in range(4):
                    gate(4 * e + i)
                if e == 0:
                    dve.wait_ge(mo_wT, 1)
                    link(v.tensor_copy(wT[:], psum[:, 6, 0:TILES * E].rearrange("p (t e) -> p t e", e=E)))
                else:
                    dve.wait_ge(mo_acc, 2 * e)
                for c in range(2):
                    dve.wait_ge(mo_y, 2 * e + c + 1)
                    for i in range(4):
                        t = 4 * c + i
                        last = v.scalar_tensor_tensor(out=acc[:, t, :], in0=psum[:, 4 + c, i * P:(i + 1) * P],
                                                      scalar=wT[:, t, e:e + 1], in1=acc[:, t, :],
                                                      op0=ALU.mult, op1=ALU.add)
                    last.then_inc(mo_acc, 1)
            dve.wait_ge(mo_acc, 2 * E)
            norm(first + 2, lambda t: acc[:, t, :], TILES, 1e-5, 0.0, lambda t: yout[:, t, :], out_ready)


def kernel(**inputs):
    import numpy as np
    import concourse.bacc as bacc
    from concourse.bass_utils import run_bass_kernel_spmd as run

    def f(name):
        return np.ascontiguousarray(inputs[name])

    x, ctx = f("x"), f("ctx_1024")
    Wq, Wk, Wv, Wo = (f("L0_xattn_W" + c) for c in "qkvo")
    by_pair = lambda w: w.reshape(L, D, PAIRS, P).transpose(0, 2, 1, 3)
    turned = lambda w: w.reshape(L, D, PAIRS, P).transpose(0, 2, 3, 1)
    wo_apart = np.zeros((L, PAIRS, 2, HD, 2, D), np.float32)
    for h in range(2):
        wo_apart[:, :, h, :, h, :] = Wo.reshape(L, PAIRS, 2, HD, D)[:, :, h]
    wpair = np.concatenate([by_pair(Wq), turned(Wk), turned(Wv), wo_apart.reshape(L, PAIRS, P, 2 * D)], axis=3)
    steps = [s // B % L for s in range(STEPS + 1)]
    W1, W3, W2 = f("L0_ffn_W1"), f("L0_ffn_W3"), f("L0_ffn_W2")
    W2T = W2.transpose(0, 2, 1).reshape(E, 2, P, D).transpose(0, 2, 1, 3).reshape(E, P, 2 * D)

    pos = np.arange(S, dtype=np.float32)
    freq = np.exp(-np.float32(np.log(10000.0)) * np.arange(0, SHD, 2, dtype=np.float32) / np.float32(SHD))
    angle = np.repeat(pos[:, None] * freq[None, :].astype(np.float32), 2, axis=1)
    sign = np.tile(np.array([-1.0, 1.0], np.float32), SHD // 2)
    wide = lambda a: np.tile(a.astype(np.float32), (1, 2 * SH)).reshape(FT, P, 2 * D).transpose(1, 0, 2)
    upper = np.where(np.arange(P)[None, :] > np.arange(P)[:, None], 1e30, 0.0).astype(np.float32)
    cmask = np.concatenate([upper, np.zeros((P, P), np.float32), upper], axis=1)
    hmask = np.where(np.arange(P)[:, None] // SHD == np.arange(SH)[None, :], -float(SHD) ** -0.5, 0.0)

    arrays = {
        "x": x, "xT": x.transpose(0, 2, 1), "fside": f("fside_BxSxS2_0"),
        "mask": f("mask_Bx1x1xS2_ff0").reshape(B, 1, T), "ctxT": ctx.transpose(0, 2, 1), "ctx": ctx,
        "wqkvT": f("L0_attn_Wqkv").T, "woT": f("L0_attn_Wo").T,
        "wpair": wpair.reshape(L * PAIRS, P, 5, P),
        "wth": f("L0_xattn_Wth").reshape(L, HID)[steps].reshape(1, -1),
        "bth": f("L0_xattn_bth")[steps].reshape(1, -1),
        "wto": f("L0_xattn_Wto").reshape(L, HID)[steps].reshape(1, -1),
        "bto": f("L0_xattn_bto").reshape(L)[steps].reshape(1, -1),
        "wf1": f("L0_xattn_Wf1"), "wf2": f("L0_xattn_Wf2").reshape(L, FB, P, D).transpose(0, 2, 1, 3),
        "bf1": f("L0_xattn_bf1").reshape(L, FB, P).transpose(0, 2, 1), "bf2": f("L0_xattn_bf2").reshape(L, 1, D),
        "wgT": f("L0_ffn_Wg").T,
        "wexp": np.concatenate([W1.transpose(0, 2, 1), W3.transpose(0, 2, 1), W2T], axis=2),
        "ident": np.eye(P, dtype=np.float32), "hmask": hmask.astype(np.float32), "cmask": cmask,
        "cos": wide(np.cos(angle)), "sin": wide(np.sin(angle) * sign),
    }
    arrays = {n: np.ascontiguousarray(a) for n, a in arrays.items()}
    nc = bacc.Bacc("TRN2", target_bir_lowering=False, num_devices=1)
    d = {n: nc.dram_tensor("in_" + n, a.shape, F32, kind="ExternalInput").ap() for n, a in arrays.items()}
    d["out"] = nc.dram_tensor("out", (B, S, D), F32, kind="ExternalOutput").ap()
    build(nc, d)
    return run(nc, [{"in_" + n: a for n, a in arrays.items()}], core_ids=[0]).results[0]["out"]
```

```python
from contextlib import ExitStack

import concourse.bass as bass
from concourse import mybir

F32 = mybir.dt.float32
F32R = mybir.dt.float32r
ALU = mybir.AluOpType
ACT = mybir.ActivationFunctionType

P = 128
B, S, D, T = 4, 256, 128, 1601
FT = S // P
L, HEADS, HD, HID = 4, 16, 64, 32
STEPS = L * B
PAIRS = HEADS // 2
UNITS = HEADS * FT
TT = -(-T // P)
LAST = T - (TT - 1) * P
TE = T + T % 2
TG = 4
CUT = 1024
FILT, FB = 512, 4
SH, SHD, GH = 16, 8, 4
SG = SH // GH
E, EH, CAP = 8, 256, 128
TOK = B * S
TILES = TOK // P
BIG = 3.0e38

START = ["XN1", "Q0", "QK0"]
OPENING = [(None, "VO", "Q"), (None, "QK0"), ("PV",), ("PV",)]
MIDDLE = [("PV", "VO", "Q"), ("PV", "QK"), ("PV", "OT"), ("PV", "Y")]
FINAL = [("PV", "VO"), ("PV", "XN1"), ("PV", "Q", "OT"), ("PV", "QK", "Y")]
SECOND = [("PV", "VO", "Q", "XN2"), ("PV", "QK", "H0"), ("PV", "OT", "H1"), ("PV", "Y", "Y2", "Y3")]


def flat(kind):
    return [name for slot in kind for name in slot if name]


AHEAD = 2
PER_PAIR = len(flat(MIDDLE))
OPENED = len(START) + len(flat(OPENING)) + PER_PAIR
AT_FINAL = PER_PAIR * (PAIRS - 1 - AHEAD)
AT_FIRST = AT_FINAL + len(flat(FINAL))
AT_SECOND = AT_FIRST + PER_PAIR
TASKS = AT_SECOND + len(flat(SECOND))
assert TASKS % 2 == 0
FIRST_BATCH = 0
HBANKS = (4, 6, 0, 2)
NORMS = 2
CHAIN_SA = 3 + 4
CHAIN_STEP = 2 * 4 + 1


def task_number(s, local):
    return OPENED + s * TASKS + local


def opening(emit):
    first = len(START)
    emit(0, 0, 0, OPENING, first, first % 2, first - 1)
    second = first + len(flat(OPENING))
    emit(0, 1, 1, MIDDLE, second, second % 2, first + flat(OPENING).index("QK0"))


def turn_of(s, emit, each_j):
    def one(step, p, parity, kind, local, odd, qk_local):
        emit(step, p, parity, kind, task_number(s, local), (OPENED + odd) % 2, task_number(s, qk_local))

    qk = flat(MIDDLE).index("QK")
    with each_j(0, (PAIRS - 1 - AHEAD) // 2) as j:
        for half in range(2):
            one(s, 2 * j + AHEAD + half, half, MIDDLE, 2 * PER_PAIR * j + PER_PAIR * half, PER_PAIR * half,
                2 * PER_PAIR * j + PER_PAIR * (half - 1) + qk)
    one(s, PAIRS - 2, 0, MIDDLE, AT_FINAL - PER_PAIR, AT_FINAL - PER_PAIR, AT_FINAL - 2 * PER_PAIR + qk)
    one(s, PAIRS - 1, 1, FINAL, AT_FINAL, AT_FINAL, AT_FINAL - PER_PAIR + qk)
    one(s + 1, 0, 0, MIDDLE, AT_FIRST, AT_FIRST, AT_FINAL + flat(FINAL).index("QK"))
    one(s + 1, 1, 1, SECOND, AT_SECOND, AT_SECOND, AT_FIRST + qk)


def pair_of(name, p, parity):
    if name in ("Q", "QK", "QK0"):
        return p + 1, 1 - parity
    if name in ("OT", "Y"):
        return p - 1, 1 - parity
    return p, parity


def weights_row(s, p):
    step, pair = (s, p) if p < PAIRS else (s + 1, p - PAIRS)
    return (step // B * PAIRS + pair) % (L * PAIRS)


def build(nc, d):
    with ExitStack() as ctx:
        def sb(name, shape):
            return ctx.enter_context(nc.sbuf_tensor(name, shape, F32))

        def sem(name):
            return ctx.enter_context(nc.semaphore(name))

        psum = ctx.enter_context(nc.psum_tensor("banks", [P, 8, 512], F32))

        ident = sb("ident", [P, P])
        half = sb("half", [P, 8])
        coef = sb("coef", [P, 2, (STEPS + 2) * HID])
        negc = sb("negc", [P, (STEPS + 2) * HID])
        nbto = sb("nbto", [P, STEPS + 2])
        xs = sb("xs", [P, B, FT, D])
        x_sa = sb("x_sa", [P, B, FT, D])
        dist = sb("dist", [P, 2, FT, T])
        maskb = sb("maskb", [P, T])
        relu = sb("relu", [P, 2, FT, T])
        nb_next = sb("nb_next", [P, FT, T])
        nb_cur = sb("nb_cur", [P, FT, T])
        ctxT = sb("ctxT", [P, 2, 2, TE])
        ctxT_in = sb("ctxT_in", [P, T])
        prob = sb("prob", [P, 2, T])
        probT = sb("probT", [P, 2, TT, P])
        ctxN = sb("ctxN", [P, 2, TT, P])
        wpair = sb("wpair", [P, 2, 5, P])
        vo = sb("vo", [P, 2, 2, P])
        wf1 = sb("wf1", [P, FILT])
        wf2 = sb("wf2", [P, FB, D])
        bf1 = sb("bf1", [P, FB])
        bf2 = sb("bf2", [P, D])
        xcur = sb("xcur", [P, FT, D])
        xmid = sb("xmid", [P, FT, D])
        xn = sb("xn", [P, FT, D])
        xnT = sb("xnT", [P, 2, S])
        q_sb = sb("q_sb", [P, 2, S])
        qk_sb = sb("qk_sb", [P, 2, 2, 2, S])
        nmA = sb("nmA", [P, 4])
        nm = sb("nm", [P, 4])
        rsum = sb("rsum", [P, 4])
        rinv = sb("rinv", [P, 4])
        On = sb("On", [P, 2, 4, P])
        OT = sb("OT", [P, 4, P])
        hT = sb("hT", [P, FB, S])
        bn = sb("bn", [P, TILES, 6])
        mv = sb("mv", [P, TILES, 2])
        vv = sb("vv", [P, TILES])
        sd = sb("sd", [P, TILES])
        rs = sb("rs", [P, TILES])

        def sems(*names):
            return [sem(n) for n in names]

        (const_ld, coef_ld, x_ld, xT_ld, out_st) = sems("const_ld", "coef_ld", "x_ld", "xT_ld", "out_st")
        (dist_ld, gate_ld, sa_ri, mo_n, carried) = sems("dist_ld", "gate_ld", "sa_ri", "mo_n", "carried")
        w_ld = sems("w_ld0", "w_ld1")
        (mask_ld, ctxT_ld, ctxN_ld, ffn_ld) = sems("mask_ld", "ctxT_ld", "ctxN_ld", "ffn_ld")
        (ctxT_high, ctxT_split, qk_high, x_kept) = sems("ctxT_high", "ctxT_split", "qk_high", "x_kept")
        exp_ld = sems("expert_ld0", "expert_ld1")
        w2_ld = sem("w2_ld")
        (half_set, nmask_done, nb_copied, dve_chain, var_ready, std_ready, x_written,
         xn_done) = sems("half_set", "nmask_done", "nb_copied", "dve_chain", "var_ready",
                         "std_ready", "x_written", "xn_done")
        (scores, scored, exped, turned, turn_copied, on_done, rinv_done, mm, mm_copied,
         relu_done, term_done) = sems("scores", "scored", "exped", "turned", "turn_copied",
                                      "on_done", "rinv_done", "mm", "mm_copied", "relu_done", "term_done")
        (sa_qkv, sa_rope, sa_turned, sa_qm, sa_scores, sa_scored, sa_exp, sa_pT, sa_pTc,
         sa_pv, sa_on, sa_oT, sa_oTc, sa_y) = sems(
            "sa_qkv", "sa_rope", "sa_turned", "sa_qm", "sa_scores", "sa_scored", "sa_exp", "sa_pT",
            "sa_pTc", "sa_pv", "sa_on", "sa_oT", "sa_oTc", "sa_y")
        sa_added = sem("sa_added")
        (mo_x, mo_xT, mo_xTc, mo_sc, mo_scc, mo_max, mo_e, mo_w, mo_wT, mo_h, mo_sil, mo_g, mo_y,
         mo_acc, out_ready) = sems(
            "mo_x", "mo_xT", "mo_xTc", "mo_sc", "mo_scc", "mo_max", "mo_e", "mo_w", "mo_wT", "mo_h",
            "mo_sil", "mo_g", "mo_y", "mo_acc", "out_ready")

        flatD1 = dist[:, 1].rearrange("p a b -> p (a b)")
        cos = flatD1[:, 0:4 * D].rearrange("p (a b) -> p a b", a=FT)
        sin = flatD1[:, 4 * D:8 * D].rearrange("p (a b) -> p a b", a=FT)
        wqkvT = flatD1[:, 8 * D:11 * D]
        woT = flatD1[:, 11 * D:12 * D]
        cmask = flatD1[:, 12 * D:15 * D]
        sa_xT = flatD1[:, 15 * D:17 * D]
        hmask = sb("hmask", [P, SH])
        flatT = probT[:, :, :, :].rearrange("p a b c -> p (a b c)")
        flatV = ctxN[:, :, :, :].rearrange("p i a b -> p (i a b)")
        qkr = flatT[:, 0:512].rearrange("p (a b) -> p a b", a=2)
        rot1 = flatT[:, 512:1024].rearrange("p (a b) -> p a b", a=2)
        rot2 = flatT[:, 1024:1536].rearrange("p (a b) -> p a b", a=2)
        qkT = flatT[:, 1536:2048].rearrange("p (a b) -> p a b", a=2)
        o_sa = flatT[:, 2048:2304].rearrange("p (a b) -> p a b", a=2)
        oT_sa = flatT[:, 2304:2560]
        v_sa = flatT[:, 2560:3072].rearrange("p (i a b) -> p i a b", i=2, a=FT)
        qm = flatV[:, 0:2048].rearrange("p (i a b) -> p i a b", i=2, a=GH)
        s_sa = prob[:, :, 0:1536].rearrange("p i (a b) -> p i a b", a=GH)
        pT_sa = nb_cur[:, 0, 0:1536].rearrange("p (a b) -> p a b", a=GH)
        nm_sa = sb("nm_sa", [P, 2, 2, GH])
        rs_sa = sb("rs_sa", [P, 2, 2, GH])
        ri_sa = sb("ri_sa", [P, 2, GH])

        flatR = relu[:, :, :, :].rearrange("p a b c -> p (a b c)")
        flatD = dist[:, :, :, :].rearrange("p a b c -> p (a b c)")
        x2T = flatR[:, 0:TOK]
        sil = flatR[:, TOK:2 * TOK].rearrange("p (a b) -> p a b", a=2)
        x2 = flatD[:, 0:TOK].rearrange("p (a b) -> p a b", a=TILES)
        yout = x2
        acc = flatD[:, TOK:2 * TOK].rearrange("p (a b) -> p a b", a=TILES)
        w13 = flatD[:, 2 * TOK:2 * TOK + 4 * EH].rearrange("p (a b) -> p a b", a=2)
        wgT = flatD[:, 3 * TOK:3 * TOK + E]
        w2 = flatD[:, 4 * TOK:4 * TOK + E * EH].rearrange("p (a b) -> p a b", a=E)
        flatN = nb_next[:, :, :].rearrange("p a b -> p (a b)")
        flatC = nb_cur[:, :, :].rearrange("p a b -> p (a b)")
        flatP = prob[:, :, :].rearrange("p a b -> p (a b)")
        rooms = ((flatR, 2, 6), (flatP, 0, 3), (flatT, 0, 3), (flatV, 0, 3), (flatC, 0, 3))
        gat = [room[:, i * TOK:(i + 1) * TOK] for room, lo, hi in rooms for i in range(lo, hi)]
        sc8 = flatN[0:E, 0:TOK]
        work = flatN[0:E, TOK:2 * TOK]
        ex8 = flatN[0:E, 2 * TOK:3 * TOK]
        keep = hT[0:E, :, :].rearrange("p a b -> p (a b)")
        w8 = On[0:E, :, :, :].rearrange("p a b c -> p (a b c)")
        top8 = sb("top8", [E, 8])
        sm8 = sb("sm8", [E, 4])
        tick = sb("tick", [P, 1])
        wT = sb("wT", [P, TILES, E])

        x_tiles = d["x"].rearrange("b (t p) d -> p b t d", p=P)
        f_tiles = d["fside"].rearrange("b (t p) k -> b p t k", p=P)

        def tiles_of(g):
            return range(4 * g, min(4 * g + 4, TT))

        def rows_of(t):
            return P if t < TT - 1 else LAST

        block = ctx.enter_context(nc.Block())

        def apart(eng):
            eng.sem_inc(carried, 1)

        @block.sync
        def _(sp):
            sp.sem_inc(scored, 2)
            sp.sem_inc(turned, 2 * TG)
            sp.sem_inc(turn_copied, 2)
            sp.sem_inc(on_done, 4)
            sp.sem_inc(mm_copied, 2)
            sp.sem_inc(term_done, 2)
            sp.sem_inc(sa_added, 1)
            for dst, name in ((ident[:], "ident"), (wqkvT, "wqkvT"), (woT, "woT"), (hmask[:], "hmask"),
                              (cmask, "cmask"), (cos, "cos"), (sin, "sin")):
                sp.dma_start(dst, d[name]).then_inc(const_ld, 16)
            for dst, name in ((coef[:, 0], "wth"), (coef[:, 1], "bth"), (negc[:], "wto"), (nbto[:], "bto")):
                sp.dma_start(dst, d[name].to_broadcast(dst.shape)).then_inc(coef_ld, 16)
            sp.dma_start(xs[:], x_tiles).then_inc(x_ld, 16)
            sp.dma_start(maskb[:], d["mask"][0].to_broadcast([P, T])).then_inc(mask_ld, 16)
            sp.dma_start(dist[:, 0], f_tiles[0]).then_inc(dist_ld, 16)
            sp.wait_ge(nmask_done, 1)
            sp.dma_start(maskb[:], d["mask"][1].to_broadcast([P, T])).then_inc(mask_ld, 16)
            for b in range(B):
                if b >= 1:
                    sp.wait_ge(sa_qkv, FT * b)
                sp.dma_start(sa_xT, d["xT"][b]).then_inc(xT_ld, 16)
            sp.wait_ge(x_written, B)
            sp.wait_ge(dist_ld, 16)
            sp.dma_start(dist[:, 1], f_tiles[1]).then_inc(dist_ld, 16)
            for p in range(2):
                sp.dma_start(wpair[:, p], d["wpair"][p]).then_inc(w_ld[p], 16)

            def load_ctxT(s):
                sp.dma_start(ctxT_in[:], d["ctxT"][s % B]).then_inc(ctxT_ld, 16)

            def load_ctxN(s, parity):
                rows = d["ctx"][s % B]
                whole = (TT - 1) * P
                sp.dma_start(ctxN[:, parity, 0:TT - 1], rows[0:whole].rearrange("(t p) d -> p t d", p=P)
                             ).then_inc(ctxN_ld, 16)
                sp.dma_start(ctxN[0:LAST, parity, TT - 1], rows[whole:T]).then_inc(ctxN_ld, 16)

            def load_ffn(s):
                layer = s // B % L
                for dst, name in ((wf1, "wf1"), (wf2, "wf2"), (bf1, "bf1")):
                    sp.dma_start(dst[:], d[name][layer]).then_inc(ffn_ld, 16)
                sp.dma_start(bf2[:], d["bf2"][layer].to_broadcast([P, D])).then_inc(ffn_ld, 16)

            def load_weights(s, p, number, half):
                sp.wait_ge(mm, number + 1)
                apart(sp)
                sp.dma_start(wpair[:, half], d["wpair"][weights_row(s, p)]).then_inc(w_ld[half], 16)

            load_ctxT(0)
            load_ctxN(0, 0)
            load_ffn(0)
            sp.wait_ge(term_done, HID + 3)
            sp.dma_start(maskb[:], d["mask"][2 % B].to_broadcast([P, T])).then_inc(mask_ld, 16)
            load_weights(0, 2, len(START) + flat(OPENING).index("VO"), 0)
            load_weights(0, 3, OPENED - PER_PAIR + flat(MIDDLE).index("VO"), 1)
            with sp.Fori(0, STEPS) as s:
                starts = [PER_PAIR * i for i in range(PAIRS - AHEAD)] + [AT_FIRST, AT_SECOND]
                for i, at in enumerate(starts):
                    name = FINAL if at == AT_FINAL else SECOND if at == AT_SECOND else MIDDLE
                    load_weights(s, AHEAD + i + 2, task_number(s, at + flat(name).index("VO")), i % 2)
                    if i == 0:
                        sp.wait_ge(ctxT_split, s + 1)
                        apart(sp)
                        load_ctxT(s + 1)
                    elif i == 1:
                        sp.wait_ge(mm, task_number(s, 0))
                        apart(sp)
                        load_ctxN(s + 1, (s + 1) % 2)
                    elif i == 2:
                        sp.wait_ge(relu_done, HID * (s + 1))
                        apart(sp)
                        sp.dma_start(dist[:, s % 2], f_tiles[(s + 2) % B]).then_inc(dist_ld, 16)
                    elif at == AT_FIRST:
                        sp.wait_ge(term_done, HID * (s + 2) + 3)
                        apart(sp)
                        sp.dma_start(maskb[:], d["mask"][(s + 3) % B].to_broadcast([P, T])).then_inc(mask_ld, 16)
                sp.wait_ge(x_written, B + s + 1)
                apart(sp)
                load_ffn(s + 1)

            sp.wait_ge(mo_x, 1)
            sp.dma_start(wgT, d["wgT"]).then_inc(gate_ld, 16)
            for e in range(2):
                sp.dma_start(w13[:, e], d["wexp"][e, :, 0:2 * EH]).then_inc(exp_ld[e], 16)
            sp.dma_start(w2, d["wexp"][:, :, 2 * EH:3 * EH].rearrange("e p c -> p e c")).then_inc(w2_ld, 16)
            for e in range(2, E):
                sp.wait_ge(mo_h, 4 * (e - 1))
                sp.dma_start(w13[:, e % 2], d["wexp"][e, :, 0:2 * EH]).then_inc(exp_ld[e % 2], 16)
            sp.wait_ge(out_ready, 1)
            sp.dma_start(d["out"].rearrange("b (t p) d -> p (b t) d", p=P), yout).then_inc(out_st, 16)
            sp.wait_ge(out_st, 16)
            sp.wait_ge(ctxT_ld, 16 * (STEPS + 1))
            sp.wait_ge(ctxN_ld, 16 * 2 * (STEPS + 1))
            sp.wait_ge(ffn_ld, 16 * 4 * (STEPS + 1))
            for ld in w_ld:
                sp.wait_ge(ld, 16 * (STEPS * PAIRS // 2 + 2))
            sp.wait_ge(mask_ld, 16 * (STEPS + 3))

        @block.gpsimd
        def _(pool):
            nc.gpsimd.memset(ctxT[:, :, :, T:TE], 0.0)
            nc.gpsimd.memset(half[:], 0.5).then_inc(half_set, 1)
            pool.wait_ge(half_set, 1)

            def root(n, width):
                pool.wait_ge(var_ready, n + 1)
                nc.gpsimd.tensor_tensor(sd[:, 0:width], vv[:, 0:width], half[:, 0:width], ALU.pow
                                        ).then_inc(std_ready, 1)

            def split_ctxT(s, parity):
                high, low = ctxT[:, parity, 0, 0:T], ctxT[:, parity, 1, 0:T]
                pool.wait_ge(ctxT_ld, 16 * (s + 1))
                nc.gpsimd.tensor_copy(high.bitcast(F32R), ctxT_in[:]).then_inc(ctxT_high, 1)
                pool.wait_ge(ctxT_high, s + 1)
                nc.gpsimd.tensor_tensor(low.bitcast(F32R), ctxT_in[:], high, ALU.subtract).then_inc(ctxT_split, 1)

            with pool.Fori(0, B) as n:
                root(n, FT)
            root(B, FT)
            split_ctxT(0, 0)
            with pool.Fori(0, STEPS) as s:
                pool.wait_ge(scores, 2 * UNITS * s + 2)
                split_ctxT(s + 1, (s + 1) % 2)
                for i in range(NORMS):
                    root(B + 1 + NORMS * s + i, FT)
            for n in range(3):
                root(B + 1 + NORMS * STEPS + n, TILES)

        @block.tensor
        def _(pe):
            mat = nc.tensor.matmul

            def turn(out, in_, k=P):
                return nc.tensor.transpose(out, in_, ident[0:k, 0:k])

            pe.wait_ge(const_ld, 16 * 7)

            def sa_project(b):
                pe.wait_ge(xT_ld, 16 * (b + 1))
                if b is not FIRST_BATCH:
                    pe.wait_ge(sa_scored, 2 * GH * SG * b)
                for ft in range(FT):
                    mat(psum[:, ft, 0:3 * D], sa_xT[:, ft * P:(ft + 1) * P], wqkvT, start=True, stop=True
                        ).then_inc(sa_qkv, 1)

            def sa_turn(b):
                pe.wait_ge(sa_rope, b + 1)
                for a in range(2):
                    for ft in range(FT):
                        last = turn(psum[:, 2, (2 * a + ft) * P:(2 * a + ft + 1) * P], qkr[:, ft, a * D:(a + 1) * D])
                last.then_inc(sa_turned, 1)

            def sa_head_scores(b, g):
                for h in range(GH):
                    pe.wait_ge(sa_qm, GH * (b * SG + g) + h + 1)
                    mat(psum[:, h, 0:P], qm[:, g % 2, h, 0:P], qkT[:, 1, 0:P], start=True, stop=True)
                    mat(psum[:, h, P:3 * P], qm[:, g % 2, h, P:2 * P], qkT[:, 1, :], start=True, stop=True
                        ).then_inc(sa_scores, 1)

            def sa_outputs(b, g):
                group = b * SG + g
                for h in range(GH):
                    pe.wait_ge(sa_exp, GH * group + h + 1)
                    if h >= 2:
                        pe.wait_ge(sa_pTc, GH * group + h - 1)
                    for c in range(3):
                        last = turn(psum[:, 4 + h % 2, c * P:(c + 1) * P], s_sa[:, g % 2, h, c * P:(c + 1) * P])
                    last.then_inc(sa_pT, 1)
                pe.wait_ge(sa_pTc, GH * group + GH)
                if g == 0:
                    pe.wait_ge(sa_added, b + 1)
                else:
                    pe.wait_ge(sa_on, group)
                for h in range(GH):
                    vs = [v_sa[:, b % 2, ft, (g * GH + h) * SHD:(g * GH + h + 1) * SHD] for ft in range(FT)]
                    o = [psum[:, 7, (a * GH + h) * SHD:(a * GH + h + 1) * SHD] for a in range(2)]
                    mat(o[0], pT_sa[:, h, 0:P], vs[0], start=True, stop=True)
                    mat(o[1], pT_sa[:, h, P:2 * P], vs[0], start=True, stop=False)
                    last = mat(o[1], pT_sa[:, h, 2 * P:3 * P], vs[1], start=False, stop=True)
                last.then_inc(sa_pv, 1)

            def sa_batch(b, more):
                for g in range(SG):
                    if g < SG - 1:
                        sa_head_scores(b, g + 1)
                    elif more:
                        sa_project(b + 1)
                    sa_outputs(b, g)
                if more:
                    sa_turn(b + 1)
                    sa_head_scores(b + 1, 0)
                pe.wait_ge(sa_on, (b + 1) * SG)
                for ft in range(FT):
                    last = turn(psum[:, 6, ft * P:(ft + 1) * P], o_sa[:, ft, :])
                last.then_inc(sa_oT, 1)
                pe.wait_ge(sa_oTc, b + 1)
                for ft in range(FT):
                    last = mat(psum[:, 7, ft * P:(ft + 1) * P], oT_sa[:, ft * P:(ft + 1) * P], woT,
                               start=True, stop=True)
                last.then_inc(sa_y, 1)

            sa_project(FIRST_BATCH)
            sa_turn(FIRST_BATCH)
            sa_head_scores(FIRST_BATCH, 0)
            with pe.Fori(0, B - 1) as b:
                sa_batch(b, True)
            sa_batch(B - 1, False)

            def task(kind, s, n, bank, p, parity):
                ps = psum[:, bank, :]
                pe.wait_ge(mm_copied, n + (2 if kind in ("Q0", "QK0") else 1))
                if kind[0] == "X":
                    pe.wait_ge(xn_done, 1 if isinstance(s, int) else
                               NORMS * (s + 1) if kind == "XN1" else NORMS * s + 1)
                    for ft in range(FT):
                        last = turn(ps[:, ft * P:(ft + 1) * P], xn[:, ft, :])
                elif kind in ("Q", "Q0"):
                    pe.wait_ge(w_ld[parity], 16 * (s * (PAIRS // 2) + p // 2 + 1))
                    last = mat(ps[:, 0:S], wpair[:, parity, 0, :], xnT[:, 0], start=True, stop=True)
                elif kind in ("QK", "QK0"):
                    last = mat(ps, wpair[:, parity, 1, :], q_sb[:, :, :].rearrange("p h c -> p (h c)"),
                               start=True, stop=True)
                elif kind == "VO":
                    last = mat(ps[:, 0:2 * P], wpair[:, parity, 2, :],
                               wpair[:, parity, 3:5, :].rearrange("p h c -> p (h c)"), start=True, stop=True)
                elif kind == "OT":
                    pe.wait_ge(on_done, 4 + s * UNITS + 4 * (p + 1))
                    for k in range(4):
                        last = turn(ps[:, k * P:(k + 1) * P], On[:, parity, k, :])
                elif kind == "Y":
                    for ft in range(FT):
                        for h in range(2):
                            last = mat(ps[:, ft * P:(ft + 1) * P], OT[:, 2 * h + ft, :], vo[:, parity, h, :],
                                       start=(h == 0), stop=(h == 1))
                elif kind[0] == "H":
                    if kind == "H0":
                        pe.wait_ge(ffn_ld, 16 * 4 * s)
                    for i in range(2):
                        f = 2 * int(kind[1]) + i
                        last = mat(ps[:, i * S:(i + 1) * S], wf1[:, f * P:(f + 1) * P], xnT[:, 1],
                                   start=True, stop=True)
                else:
                    ft = int(kind[1]) - 2
                    for f in range(FB):
                        last = mat(ps[:, 0:P], hT[:, f, ft * P:(ft + 1) * P], wf2[:, f, :],
                                   start=(f == 0), stop=(f == FB - 1))
                last.then_inc(mm, 1)

            def unit_scores(s, u, k, parity, qk_task, of_step):
                n = s * UNITS + u
                if qk_task is not None:
                    pe.wait_ge(mm_copied, qk_task + 3)
                for c, (lo, hi) in enumerate(((0, CUT), (CUT, TE))):
                    pe.wait_ge(scored, 2 * n + c + 1)
                    for i, a in enumerate(range(lo, hi, 512)):
                        z = min(a + 512, hi)
                        for part, (qp, cp) in enumerate(((1, 0), (0, 1), (0, 0))):
                            last = mat(psum[:, 2 * c + i, 0:z - a],
                                       qk_sb[:, parity, qp, k // 2, (k % 2) * P:(k % 2 + 1) * P].bitcast(F32R),
                                       ctxT[:, of_step, cp, a:z].bitcast(F32R),
                                       start=(part == 0), stop=(part == 2))
                    last.then_inc(scores, 1)

            def unit_turn(s, u, k, groups):
                n = s * UNITS + u
                for g in groups:
                    if g == 0:
                        pe.wait_ge(exped, n + 1)
                    pe.wait_ge(turn_copied, TG * n + g + 1)
                    for i, t in enumerate(tiles_of(g)):
                        m = rows_of(t)
                        last = turn(psum[0:m, 4 + g % 2, i * P:(i + 1) * P], prob[:, k % 2, t * P:t * P + m])
                    last.then_inc(turned, 1)

            def unit_pv(s, u, k, number, bank, of_step):
                n = s * UNITS + u
                pe.wait_ge(turn_copied, TG * (n + 1) + 2)
                pe.wait_ge(mm_copied, number + 1)
                for t in range(TT):
                    m = rows_of(t)
                    last = mat(psum[:, bank, 0:P], probT[0:m, k % 2, t, :], ctxN[0:m, of_step, t, :],
                               start=(t == 0), stop=(t == TT - 1))
                last.then_inc(mm, 1)

            def pair(s, p, parity, kind, base, odd, qk_task):
                off = 0
                leads = isinstance(p, int) and p == 0
                for k in range(4):
                    u = 4 * p + k
                    if leads and k == 0:
                        pe.wait_ge(ctxT_split, s + 1)
                    unit_scores(s, u, k, parity, qk_task if k == 0 else None, s % 2)
                    if kind is not OPENING or k >= 1:
                        unit_turn(s, u - 1, (k - 1) % 4, (0, 1))
                    if kind[k][0]:
                        if leads and k == 2:
                            pe.wait_ge(ctxN_ld, 32 * (s + 1))
                        unit_pv(s, u - 2, (k - 2) % 4, base + off, 6 + (odd + off) % 2,
                                (s + 1) % 2 if leads and k < 2 else s % 2)
                        off += 1
                    if kind is not OPENING or k >= 1:
                        unit_turn(s, u - 1, (k - 1) % 4, (2, 3))
                    for name in kind[k][1:]:
                        task(name, s, base + off, 6 + (odd + off) % 2, *pair_of(name, p, parity))
                        off += 1

            for i, name in enumerate(START):
                task(name, -1, i, 6 + i % 2, PAIRS, 0)
            opening(pair)
            with pe.Fori(0, STEPS) as s:
                turn_of(s, pair, pe.Fori)

            pe.wait_ge(mo_x, 1)
            pe.wait_ge(turn_copied, TG * (STEPS * UNITS + 4 * AHEAD - 1) + 2)
            for t in range(TILES):
                last = turn(psum[:, t // 4, t % 4 * P:(t % 4 + 1) * P], x2[:, t, :])
            last.then_inc(mo_xT, 1)
            pe.wait_ge(mo_xTc, 1)
            pe.wait_ge(gate_ld, 16)
            for c in range(2):
                last = mat(psum[0:E, 2 + c, :], wgT, x2T[:, c * 512:(c + 1) * 512], start=True, stop=True)
            last.then_inc(mo_sc, 1)
            for i in range(4 * E):
                e, hh, c = i // 4, i // 2 % 2, i % 2
                if i % 4 == 0:
                    pe.wait_ge(exp_ld[e % 2], 16 * (e // 2 + 1))
                if i == 2:
                    pe.wait_ge(mo_scc, 1)
                if i >= 4:
                    pe.wait_ge(mo_g, i - 3)
                for a in range(2):
                    last = mat(psum[:, HBANKS[i % 4] + a, :], w13[:, e % 2, a * EH + hh * P:a * EH + (hh + 1) * P],
                               x2T[:, c * 512:(c + 1) * 512], start=True, stop=True)
                last.then_inc(mo_h, 1)
            pe.wait_ge(mo_g, 4 * E)
            pe.wait_ge(mo_w, 1)
            for t in range(TILES):
                last = turn(psum[:, 6, t * E:(t + 1) * E], w8[:, t * P:(t + 1) * P], E)
            last.then_inc(mo_wT, 1)
            pe.wait_ge(w2_ld, 16)
            for e in range(E):
                for c in range(2):
                    if e >= 2:
                        pe.wait_ge(mo_acc, 2 * (e - 2) + c + 1)
                    for i in range(4):
                        t = 4 * c + i
                        for hh in range(2):
                            last = mat(psum[:, 2 * (e % 2) + c, i * P:(i + 1) * P],
                                       gat[2 * e + hh][:, t * P:(t + 1) * P], w2[:, e, hh * P:(hh + 1) * P],
                                       start=(hh == 0), stop=(hh == 1))
                    last.then_inc(mo_y, 1)

        @block.scalar
        def _(act):
            fun = nc.scalar.activation

            def bias_relu(n, buf, slot):
                act.wait_ge(term_done, n + 1)
                fun(relu[:, buf], slot, ACT.Relu, bias=coef[:, 1, bass.ds(n, 1)],
                    scale=coef[:, 0, bass.ds(n, 1)]).then_inc(relu_done, 1)

            act.wait_ge(coef_ld, 16 * 4)
            act.wait_ge(dist_ld, 16)

            def sa_exps(b, g):
                for h in range(GH):
                    for a in range(2):
                        act.wait_ge(sa_scored, 2 * GH * (b * SG + g) + 2 * h + a + 1)
                        part = s_sa[:, g % 2, h, 0:P] if a == 0 else s_sa[:, g % 2, h, P:3 * P]
                        last = fun(part, part, ACT.Exp, scale=-1.0, bias=nm_sa[:, g % 2, a, h:h + 1],
                                   accum_out=rs_sa[:, g % 2, a, h:h + 1])
                    last.then_inc(sa_exp, 1)

            def sa_batch(b, more):
                for g in range(SG):
                    group = b * SG + g
                    if g < SG - 1:
                        sa_exps(b, g + 1)
                    for h in range(GH):
                        act.wait_ge(sa_pT, GH * group + h + 1)
                        fun(pT_sa[:, h, :], psum[:, 4 + h % 2, 0:3 * P], ACT.Copy).then_inc(sa_pTc, 1)
                    last = g == SG - 1 and not more
                    if not last:
                        bias_relu(2 * (group + 1), 0, dist[:, 0])
                    if g == SG - 1 and more:
                        sa_exps(b + 1, 0)
                    if not last:
                        bias_relu(2 * (group + 1) + 1, 1, dist[:, 0])

            for i in range(2):
                bias_relu(i, i, dist[:, 0])
            sa_exps(FIRST_BATCH, 0)
            with act.Fori(0, B - 1) as b:
                sa_batch(b, True)
            sa_batch(B - 1, False)

            def unit_exp(s, u, k):
                n = s * UNITS + u
                act.wait_ge(scored, 2 * n + 4)
                fun(prob[:, k % 2, :], prob[:, k % 2, :], ACT.Exp, scale=-1.0, bias=nm[:, k:k + 1],
                    accum_out=rsum[:, k:k + 1]).then_inc(exped, 1)

            def unit_copy(s, u, k, groups):
                n = s * UNITS + u
                for g in groups:
                    act.wait_ge(turned, TG * (n + 2) + g + 1)
                    if g == 0:
                        act.wait_ge(on_done, n + 3)
                    ts = tiles_of(g)
                    m = rows_of(ts[-1])
                    fun(probT[0:m, k % 2, ts[0]:ts[-1] + 1, :],
                        psum[0:m, 4 + g % 2, 0:len(ts) * P].rearrange("p (t q) -> p t q", q=P), ACT.Copy
                        ).then_inc(turn_copied, 1)

            def pair(s, p, parity, kind, base, odd, qk_task):
                if isinstance(p, int) and p == 0:
                    act.wait_ge(dist_ld, 16 * (s + 2))
                for k in range(4):
                    u = 4 * p + k
                    turned_before = kind is not OPENING or k >= 1
                    bias_relu((s + 1) * HID + u, k % 2, dist[:, (s + 1) % 2])
                    if turned_before:
                        unit_copy(s, u - 1, (k - 1) % 4, (0, 1))
                    unit_exp(s, u, k)
                    if turned_before:
                        unit_copy(s, u - 1, (k - 1) % 4, (2, 3))

            opening(pair)
            with act.Fori(0, STEPS) as s:
                turn_of(s, pair, act.Fori)

            act.wait_ge(mo_max, 1)
            fun(ex8, sc8, ACT.Exp, bias=sm8[:, 0:1]).then_inc(mo_e, 1)
            for i in range(4 * E):
                act.wait_ge(mo_h, i + 1)
                if i >= 2:
                    act.wait_ge(mo_g, i - 1)
                fun(sil[:, i % 2, :], psum[:, HBANKS[i % 4], :], ACT.Silu).then_inc(mo_sil, 1)

        @block.vector
        def _(dve):
            v = nc.vector
            chain = {"base": 0, "n": 0}

            def link(ins):
                chain["n"] += 1
                ins.then_inc(dve_chain, 1)
                dve.wait_ge(dve_chain, chain["base"] + chain["n"])

            def norm_stats(src, width, before):
                for t in range(width):
                    last = v.bn_stats(bn[:, t, :], src(t))
                link(last)
                apart(dve)
                for t in range(width):
                    last = v.bn_aggr(mv[:, t, :], bn[:, t, :])
                link(last)
                v.tensor_scalar(vv[:, 0:width], mv[:, 0:width, 1], before, None, ALU.add).then_inc(var_ready, 1)

            def norm_rest(n, src, width, after, out, done):
                dve.wait_ge(std_ready, n + 1)
                link(v.tensor_scalar(rs[:, 0:width], sd[:, 0:width], after, None, ALU.add))
                link(v.reciprocal(rs[:, 0:width], rs[:, 0:width]))
                for t in range(width):
                    last = v.tensor_scalar(out(t), src(t), mv[:, t, 0:1], rs[:, t:t + 1], ALU.subtract, ALU.mult)
                last.then_inc(done, 1)

            def norm(n, src, width, before, after, out, done):
                norm_stats(src, width, before)
                norm_rest(n, src, width, after, out, done)

            def bias_term(n, buf, first, tiles=range(FT), out=nb_next):
                if 0 in tiles:
                    dve.wait_ge(relu_done, n + 1)
                    dve.wait_ge(term_done, n + 2)
                for ft in tiles:
                    start = maskb[:, :] if first else nb_next[:, ft, :]
                    last = v.scalar_tensor_tensor(out=out[:, ft, :], in0=relu[:, buf, ft, :],
                                                  scalar=negc[:, bass.ds(n, 1)], in1=start,
                                                  op0=ALU.mult, op1=ALU.add)
                if FT - 1 in tiles:
                    last.then_inc(term_done, 1)

            v.memset(q_sb[:], 0.0)
            dve.wait_ge(coef_ld, 16 * 4)
            v.tensor_scalar(negc[:], negc[:], -1.0, None, ALU.mult)
            link(v.tensor_scalar(nbto[:], nbto[:], -1.0, None, ALU.mult))
            dve.wait_ge(mask_ld, 16)
            for ft in range(FT):
                last = v.tensor_scalar(nb_next[:, ft, :], maskb[:], -1.0, nbto[:, 0:1], ALU.mult, ALU.add)
            last.then_inc(nmask_done, 1)
            dve.wait_ge(nmask_done, 1)
            dve.wait_ge(const_ld, 16 * 7)

            def sa_rotate(b):
                dve.wait_ge(sa_qkv, FT * (b + 1))
                for ft in range(FT):
                    ps = psum[:, ft, 0:2 * D]
                    v.tensor_tensor(rot1[:, ft, :], ps, cos[:, ft, :], ALU.mult)
                    two = [x.rearrange("p (i two) -> p i two", two=2) for x in (rot2[:, ft, :], ps, sin[:, ft, :])]
                    for a in range(2):
                        last = v.tensor_tensor(two[0][:, :, a], two[1][:, :, 1 - a], two[2][:, :, a], ALU.mult)
                    v.tensor_copy(v_sa[:, b % 2, ft, :], psum[:, ft, 2 * D:3 * D])
                link(last)
                v.tensor_tensor(qkr, rot1, rot2, ALU.add).then_inc(sa_rope, 1)

            def sa_mask_queries(g):
                for h in range(GH):
                    v.tensor_scalar(qm[:, g % 2, h, :], qkT[:, 0, :], hmask[:, g * GH + h:g * GH + h + 1], None,
                                    ALU.mult).then_inc(sa_qm, 1)

            def sa_mask_scores(b, g):
                for h in range(GH):
                    dve.wait_ge(sa_scores, GH * (b * SG + g) + h + 1)
                    for a, (lo, hi) in enumerate(((0, P), (P, 3 * P))):
                        apart(dve)
                        v.tensor_tensor_reduce(out=s_sa[:, g % 2, h, lo:hi], in0=psum[:, h, lo:hi],
                                               in1=cmask[:, lo:hi], scale=1.0, scalar=BIG, op0=ALU.add,
                                               op1=ALU.min, accum_out=nm_sa[:, g % 2, a, h:h + 1]
                                               ).then_inc(sa_scored, 1)

            def sa_first_group(b):
                dve.wait_ge(sa_turned, b + 1)
                link(v.tensor_copy(qkT, psum[:, 2, :].rearrange("p (a c) -> p a c", a=2)))
                sa_mask_queries(0)
                sa_mask_scores(b, 0)
                sa_mask_queries(1)

            def sa_batch(b, more):
                chain["base"], chain["n"] = after_front + b * CHAIN_SA, 0
                for g in range(SG):
                    group = b * SG + g
                    if g < SG - 1:
                        sa_mask_scores(b, g + 1)
                        if g < SG - 2:
                            sa_mask_queries(g + 2)
                    elif more:
                        sa_rotate(b + 1)
                    bias_term(2 * group, 0, False)
                    if g < SG - 1:
                        bias_term(2 * group + 1, 1, False)
                    dve.wait_ge(sa_pv, group + 1)
                    v.reciprocal(ri_sa[:], rs_sa[:, g % 2]).then_inc(sa_ri, 1)
                    dve.wait_ge(sa_ri, group + 1)
                    lo, hi = g * GH * SHD, (g + 1) * GH * SHD
                    v.tensor_tensor(o_sa[:, :, lo:hi].rearrange("p a (h c) -> p a h c", c=SHD),
                                    psum[:, 7, 0:2 * GH * SHD].rearrange("p (a h c) -> p a h c", a=2, c=SHD),
                                    ri_sa[:].rearrange("p a (h o) -> p a h o", o=1).to_broadcast([P, 2, GH, SHD]),
                                    ALU.mult).then_inc(sa_on, 1)
                if more:
                    sa_first_group(b + 1)
                dve.wait_ge(sa_oT, b + 1)
                v.tensor_copy(oT_sa, psum[:, 6, 0:S]).then_inc(sa_oTc, 1)
                bias_term(2 * (b + 1) * SG - 1, 1, False)
                dve.wait_ge(sa_y, b + 1)
                dve.wait_ge(x_ld, 16)
                link(v.tensor_tensor(xcur[:], xs[:, b], psum[:, 7, 0:S].rearrange("p (a c) -> p a c", a=2), ALU.add))
                v.memset(tick[:], 0.0).then_inc(sa_added, 1)
                norm(b, lambda t: xcur[:, t, :], FT, 1e-5, 0.0, lambda t: xs[:, b, t, :], x_written)

            sa_rotate(FIRST_BATCH)
            sa_first_group(FIRST_BATCH)
            after_front = chain["n"]
            with dve.Fori(0, B - 1) as b:
                sa_batch(b, True)
                chain_sa = chain["n"]
            assert chain_sa == CHAIN_SA, chain_sa
            sa_batch(B - 1, False)
            after_sa = chain["base"] + chain["n"]

            def copy(kind, s, n, bank, p, parity):
                ps = psum[:, bank, :]
                dve.wait_ge(mm, n + 1)
                if kind[0] == "X":
                    last = v.tensor_copy(xnT[:, int(kind == "XN2")], ps[:, 0:S])
                elif kind in ("Q", "Q0"):
                    for h in range(2):
                        k = slice(h * HD, (h + 1) * HD)
                        last = v.tensor_scalar(q_sb[k, h, :], ps[k, 0:S], -float(HD) ** -0.5, None, ALU.mult)
                elif kind in ("QK", "QK0"):
                    high, low = (qk_sb[:, parity, i].rearrange("p h c -> p (h c)") for i in range(2))
                    v.tensor_copy(high.bitcast(F32R), ps).then_inc(qk_high, 1)
                    dve.wait_ge(qk_high, s * PAIRS + p + 1)
                    last = v.tensor_tensor(low.bitcast(F32R), ps, high, ALU.subtract)
                elif kind == "VO":
                    last = v.tensor_copy(vo[:, parity], ps[:, 0:2 * P].rearrange("p (h c) -> p h c", h=2))
                elif kind == "OT":
                    last = v.tensor_copy(OT[:], ps.rearrange("p (k c) -> p k c", k=4))
                elif kind == "Y":
                    before = xs[:, s % B] if isinstance(p, int) and p == 0 else xcur[:]
                    last = v.tensor_tensor(xcur[:], before, ps[:, 0:S].rearrange("p (a c) -> p a c", a=2), ALU.add)
                elif kind in ("Y2", "Y3"):
                    ft = int(kind[1]) - 2
                    last = v.tensor_tensor(xs[:, (s + B - 1) % B, ft], xmid[:, ft], ps[:, 0:P], ALU.add)
                elif kind[0] == "H":
                    for i in range(2):
                        f = 2 * int(kind[1]) + i
                        last = v.tensor_scalar(hT[:, f, :], ps[:, i * S:(i + 1) * S], bf1[:, f:f + 1], 0.0,
                                               ALU.add, ALU.max)
                last.then_inc(mm_copied, 1)
                if kind == "Y3":
                    v.memset(tick[:], 0.0).then_inc(x_written, 1)

            def unit_add(s, u, k, ends):
                n = s * UNITS + u
                dve.wait_ge(turned, TG * (n + 1))
                for c, (lo, hi) in enumerate(((0, CUT), (CUT, T))):
                    dve.wait_ge(scores, 2 * n + c + 1)
                    if c == 1:
                        if ends:
                            o = (k - 2) % 4
                            dve.wait_ge(exped, n - 1)
                            v.reciprocal(rinv[:, o:o + 1], rsum[:, o:o + 1]).then_inc(rinv_done, 1)
                        dve.wait_ge(scored, 2 * n + 3)
                    apart(dve)
                    v.tensor_tensor_reduce(
                        out=prob[:, k % 2, lo:hi],
                        in0=psum[:, 2 * c:2 * c + 2, :].rearrange("p a b -> p (a b)")[:, 0:hi - lo],
                        in1=nb_cur[:, k % 2, lo:hi], scale=1.0, scalar=BIG if c == 0 else nmA[:, k:k + 1],
                        op0=ALU.add, op1=ALU.min, accum_out=(nmA if c == 0 else nm)[:, k:k + 1]).then_inc(scored, 1)

            def unit_norm(s, u, k, number, bank, parity):
                n = s * UNITS + u
                dve.wait_ge(mm, number + 1)
                dve.wait_ge(rinv_done, n + 1)
                v.tensor_scalar(On[:, parity, k, :], psum[:, bank, 0:P], rinv[:, k:k + 1], None, ALU.mult
                                ).then_inc(mm_copied, 1)
                v.memset(tick[:], 0.0).then_inc(on_done, 1)

            def negate_mask(s):
                dve.wait_ge(term_done, HID * s + 2)
                dve.wait_ge(mask_ld, 16 * (s + 1))
                v.tensor_scalar(maskb[:], maskb[:], -1.0, nbto[:, bass.ds(s, 1)], ALU.mult, ALU.add
                                ).then_inc(nmask_done, 1)
                dve.wait_ge(nmask_done, s + 1)

            def pair(s, p, parity, kind, base, odd, qk_task):
                off = 0
                leads = isinstance(p, int) and p == 0
                if leads:
                    negate_mask(s + 1)
                for k in range(4):
                    u = 4 * p + k
                    unit_add(s, u, k, kind[k][0] == "PV")
                    term = ((s + 1) * HID + u, k % 2, leads and k == 0)
                    out = nb_cur if kind is FINAL and k == 3 else nb_next
                    normed = k == 0 and {id(FINAL): 1, id(SECOND): 2}.get(id(kind), 0)
                    if normed == 1:
                        dve.wait_ge(x_written, s + 2)
                        source = xs[:, (s + 1) % B]
                    elif normed == 2:
                        dve.wait_ge(mm_copied, base + 2)
                        source = xcur
                    if normed:
                        norm_stats(lambda t: source[:, t, :], FT, 0.0)
                    bias_term(*term, [0], out)
                    if normed:
                        norm_rest(B + NORMS * s + normed % 2, lambda t: source[:, t, :], FT, 1e-6,
                                  lambda t: xn[:, t, :], xn_done)
                    if normed == 2:
                        dve.wait_ge(ffn_ld, 16 * 4 * s)
                        link(v.tensor_tensor(xmid[:], xcur[:],
                                             bf2[:].rearrange("p (o c) -> p o c", o=1).to_broadcast([P, FT, D]),
                                             ALU.add))
                    for name in kind[k]:
                        if name == "PV":
                            unit_norm(s, u - 2, (k - 2) % 4, base + off, 6 + (odd + off) % 2,
                                      parity if k >= 2 else 1 - parity)
                        elif name:
                            copy(name, s, base + off, 6 + (odd + off) % 2, *pair_of(name, p, parity))
                        off += 1 if name else 0
                    bias_term(*term, [1], out)

            chain["base"], chain["n"] = after_sa, 0
            dve.wait_ge(x_written, B)
            v.tensor_copy(x_sa[:], xs[:]).then_inc(x_kept, 1)
            norm(B, lambda t: xs[:, 0, t, :], FT, 0.0, 1e-6, lambda t: xn[:, t, :], xn_done)
            dve.wait_ge(term_done, HID + 2)
            v.tensor_copy(nb_cur[:], nb_next[:]).then_inc(nb_copied, 1)
            dve.wait_ge(nb_copied, 1)
            for i, name in enumerate(START):
                copy(name, -1, i, 6 + i % 2, PAIRS, 0)
            opening(pair)
            after_opening = after_sa + chain["n"]
            with dve.Fori(0, STEPS) as s:
                chain["base"], chain["n"] = after_opening + s * CHAIN_STEP, 0
                turn_of(s, pair, dve.Fori)
                chain_step = chain["n"]
            assert chain_step == CHAIN_STEP, chain_step
            chain["base"], chain["n"] = after_opening + STEPS * CHAIN_STEP, 0

            first = B + 1 + NORMS * STEPS
            dve.wait_ge(x_written, B + STEPS)
            dve.wait_ge(dist_ld, 16 * (STEPS + 2))
            dve.wait_ge(relu_done, HID * (STEPS + 1) + 4 * AHEAD)
            dve.wait_ge(x_kept, 1)
            dve.wait_ge(exped, STEPS * UNITS + 4 * AHEAD)
            norm(first, lambda t: xs[:, t // FT, t % FT, :], TILES, 0.0, 1e-6, lambda t: x2[:, t, :], mo_n)
            dve.wait_ge(mo_n, 1)
            link(v.tensor_tensor(acc.rearrange("p t d -> p (t d)"), x2.rearrange("p t d -> p (t d)"),
                                 x_sa[:].rearrange("p b t d -> p (b t d)"), ALU.add))
            norm(first + 1, lambda t: acc[:, t, :], TILES, 1e-5, 0.0, lambda t: x2[:, t, :], mo_x)
            dve.wait_ge(mo_x, 1)
            link(v.tensor_copy(acc, x2))

            dve.wait_ge(mo_xT, 1)
            v.tensor_copy(x2T, psum[:, 0:2, :].rearrange("p a b -> p (a b)")).then_inc(mo_xTc, 1)
            dve.wait_ge(mo_sc, 1)
            v.tensor_copy(sc8, psum[0:E, 2:4, :].rearrange("p a b -> p (a b)"))
            link(v.tensor_copy(work, psum[0:E, 2:4, :].rearrange("p a b -> p (a b)")))

            def gate(i):
                dve.wait_ge(mo_sil, i + 1)
                v.tensor_tensor(gat[i // 2][:, i % 2 * 512:(i % 2 + 1) * 512], sil[:, i % 2, :],
                                psum[:, HBANKS[i % 4] + 1, :], ALU.mult).then_inc(mo_g, 1)

            assert 2 * (CAP // 8) == 4 * E
            for r in range(CAP // 8):
                link(v.max(top8[:], work))
                if r == 0:
                    v.tensor_scalar(sm8[:, 0:1], top8[:, 0:1], -1.0, None, ALU.mult).then_inc(mo_max, 1)
                    v.memset(tick[:], 0.0).then_inc(mo_scc, 1)
                gate(2 * r)
                link(v.match_replace(out=work, in_to_replace=top8[:], in_values=work, imm_value=-BIG))
                gate(2 * r + 1)
            link(v.tensor_tensor(keep, work, sc8, ALU.not_equal))
            dve.wait_ge(mo_e, 1)
            link(v.tensor_tensor_reduce(out=w8, in0=ex8, in1=keep, scale=1.0, scalar=0.0, op0=ALU.mult,
                                        op1=ALU.add, accum_out=sm8[:, 1:2]))
            link(v.reciprocal(sm8[:, 2:3], sm8[:, 1:2]))
            v.tensor_scalar(w8, w8, sm8[:, 2:3], None, ALU.mult).then_inc(mo_w, 1)

            dve.wait_ge(mo_wT, 1)
            link(v.tensor_copy(wT[:], psum[:, 6, 0:TILES * E].rearrange("p (t e) -> p t e", e=E)))
            for e in range(E):
                if e >= 1:
                    dve.wait_ge(mo_acc, 2 * e)
                for c in range(2):
                    dve.wait_ge(mo_y, 2 * e + c + 1)
                    for i in range(4):
                        t = 4 * c + i
                        last = v.scalar_tensor_tensor(out=acc[:, t, :], in0=psum[:, 2 * (e % 2) + c, i * P:(i + 1) * P],
                                                      scalar=wT[:, t, e:e + 1], in1=acc[:, t, :],
                                                      op0=ALU.mult, op1=ALU.add)
                    last.then_inc(mo_acc, 1)
            dve.wait_ge(mo_acc, 2 * E)
            norm(first + 2, lambda t: acc[:, t, :], TILES, 1e-5, 0.0, lambda t: yout[:, t, :], out_ready)


def kernel(**inputs):
    import numpy as np
    import concourse.bacc as bacc
    from concourse.bass_utils import run_bass_kernel_spmd as run

    def f(name):
        return np.ascontiguousarray(inputs[name])

    x, ctx = f("x"), f("ctx_1024")
    Wq, Wk, Wv, Wo = (f("L0_xattn_W" + c) for c in "qkvo")
    by_pair = lambda w: w.reshape(L, D, PAIRS, P).transpose(0, 2, 1, 3)
    turned = lambda w: w.reshape(L, D, PAIRS, P).transpose(0, 2, 3, 1)
    wo_apart = np.zeros((L, PAIRS, 2, HD, 2, D), np.float32)
    for h in range(2):
        wo_apart[:, :, h, :, h, :] = Wo.reshape(L, PAIRS, 2, HD, D)[:, :, h]
    wpair = np.concatenate([by_pair(Wq), turned(Wk), turned(Wv), wo_apart.reshape(L, PAIRS, P, 2 * D)], axis=3)
    steps = [s // B % L for s in range(STEPS + 2)]
    W1, W3, W2 = f("L0_ffn_W1"), f("L0_ffn_W3"), f("L0_ffn_W2")
    W2T = W2.transpose(0, 2, 1).reshape(E, 2, P, D).transpose(0, 2, 1, 3).reshape(E, P, 2 * D)

    pos = np.arange(S, dtype=np.float32)
    freq = np.exp(-np.float32(np.log(10000.0)) * np.arange(0, SHD, 2, dtype=np.float32) / np.float32(SHD))
    angle = np.repeat(pos[:, None] * freq[None, :].astype(np.float32), 2, axis=1)
    sign = np.tile(np.array([-1.0, 1.0], np.float32), SHD // 2)
    wide = lambda a: np.tile(a.astype(np.float32), (1, 2 * SH)).reshape(FT, P, 2 * D).transpose(1, 0, 2)
    upper = np.where(np.arange(P)[None, :] > np.arange(P)[:, None], 1e30, 0.0).astype(np.float32)
    cmask = np.concatenate([upper, np.zeros((P, P), np.float32), upper], axis=1)
    hmask = np.where(np.arange(P)[:, None] // SHD == np.arange(SH)[None, :], -float(SHD) ** -0.5, 0.0)

    arrays = {
        "x": x, "xT": x.transpose(0, 2, 1), "fside": f("fside_BxSxS2_0"),
        "mask": f("mask_Bx1x1xS2_ff0").reshape(B, 1, T), "ctxT": ctx.transpose(0, 2, 1), "ctx": ctx,
        "wqkvT": f("L0_attn_Wqkv").T, "woT": f("L0_attn_Wo").T,
        "wpair": wpair.reshape(L * PAIRS, P, 5, P),
        "wth": f("L0_xattn_Wth").reshape(L, HID)[steps].reshape(1, -1),
        "bth": f("L0_xattn_bth")[steps].reshape(1, -1),
        "wto": f("L0_xattn_Wto").reshape(L, HID)[steps].reshape(1, -1),
        "bto": f("L0_xattn_bto").reshape(L)[steps].reshape(1, -1),
        "wf1": f("L0_xattn_Wf1"), "wf2": f("L0_xattn_Wf2").reshape(L, FB, P, D).transpose(0, 2, 1, 3),
        "bf1": f("L0_xattn_bf1").reshape(L, FB, P).transpose(0, 2, 1), "bf2": f("L0_xattn_bf2").reshape(L, 1, D),
        "wgT": f("L0_ffn_Wg").T,
        "wexp": np.concatenate([W1.transpose(0, 2, 1), W3.transpose(0, 2, 1), W2T], axis=2),
        "ident": np.eye(P, dtype=np.float32), "hmask": hmask.astype(np.float32), "cmask": cmask,
        "cos": wide(np.cos(angle)), "sin": wide(np.sin(angle) * sign),
    }
    arrays = {n: np.ascontiguousarray(a) for n, a in arrays.items()}
    nc = bacc.Bacc("TRN2", target_bir_lowering=False, num_devices=1)
    d = {n: nc.dram_tensor("in_" + n, a.shape, F32, kind="ExternalInput").ap() for n, a in arrays.items()}
    d["out"] = nc.dram_tensor("out", (B, S, D), F32, kind="ExternalOutput").ap()
    build(nc, d)
    return run(nc, [{"in_" + n: a for n, a in arrays.items()}], core_ids=[0]).results[0]["out"]
```
